# Optimizing a Trainium2 kernel written in Bass

```python
import numpy as np
import jax
import jax.numpy as jnp

def _softmax(x, axis=-1):
    return jax.nn.softmax(x, axis=axis)

def _gelu(x):
    return jax.nn.gelu(x, approximate=True)

def _silu(x):
    return jax.nn.silu(x)

def _sigmoid(x):
    return jax.nn.sigmoid(x)

def _layernorm(x, axis=-1, eps=1e-05):
    m = jnp.mean(x, axis=axis, keepdims=True)
    v = jnp.var(x, axis=axis, keepdims=True)
    return (x - m) / jnp.sqrt(v + eps)

def _scatter_add(tgt, idx, src, axis=0):
    return tgt.at[idx].add(src)

def _segment_sum(src, seg, n):
    return jax.ops.segment_sum(src, seg, n)
kernel_name = 'mk_xattn_ffn_d1_seqx_r8_8ed88a'

def setup_inputs(seed: int=0):
    np.random.seed(seed)
    _w = jnp.asarray

    def _rec_inputs():
        import jax
        import jax.numpy as jnp
        _rk = jax.random.key(seed)
        x = 7.22e-05 + 1 * jax.random.normal(jax.random.fold_in(_rk, 1), (8, 56, 128), jnp.float32)
        _lenS = 56 - jax.random.randint(jax.random.fold_in(_rk, 7), (8,), 0, max(1, 56 // 4) + 1, jnp.int32)
        _lenS2 = 1500 - jax.random.randint(jax.random.fold_in(_rk, 8), (8,), 0, max(1, 1500 // 4) + 1, jnp.int32)
        _ctx_1024P = jax.random.normal(jax.random.fold_in(_rk, 11), (8, 16, 128), jnp.float32)
        _ctx_1024c = jax.random.dirichlet(jax.random.fold_in(_rk, 511), 0.3 * jnp.ones((16,), jnp.float32), (8, 1500))
        _ctx_1024t = jnp.einsum('bsk,bkd->bsd', _ctx_1024c, _ctx_1024P)
        _ctx_1024t = _ctx_1024t * jax.lax.rsqrt(jnp.mean(jnp.square(_ctx_1024t)) + 1e-12) * 0.953939
        ctx_1024 = 4.13588e-05 + 0.999923 * (_ctx_1024t + 0.3 * jax.random.normal(jax.random.fold_in(_rk, 611), (8, 1500, 128), jnp.float32))
        return (x, ctx_1024)
    x, ctx_1024 = _rec_inputs()

    def _L0_xattn_setup():
        import jax, jax.numpy as jnp
        import numpy as np
        DIM = 128
        HEADS = 16
        DIM_HEAD = 64
        SCALE = DIM_HEAD ** (-0.5)
        EPS = 1e-05

        def stable_layernorm(x, g):
            x = x / jax.lax.stop_gradient(jnp.max(x, axis=-1, keepdims=True))
            mean = jnp.mean(x, axis=-1, keepdims=True)
            var = jnp.mean(jnp.square(x - mean), axis=-1, keepdims=True)
            return (x - mean) * jax.lax.rsqrt(var + EPS) * g
        key = jax.random.key(seed)
        ks = jax.random.split(key, 6)
        b, n, m = (4, 256, 256)
        inner = HEADS * DIM_HEAD
        return {'x': jax.random.normal(ks[0], (b, n, DIM), jnp.float32), 'context': jax.random.normal(ks[1], (b, m, DIM), jnp.float32), 'Wq': jax.random.normal(ks[2], (DIM, inner), jnp.float32) * 0.02, 'Wkv': jax.random.normal(ks[3], (DIM, 2 * inner), jnp.float32) * 0.02, 'Wo': jax.random.normal(ks[4], (inner, DIM), jnp.float32) * 0.02, 'g_in': jnp.ones((DIM,), jnp.float32), 'g_out': jnp.ones((DIM,), jnp.float32), 'null_kv': jax.random.normal(ks[5], (2, DIM_HEAD), jnp.float32)}
    _L0_xattn_all = _L0_xattn_setup()
    _L0_xattn_in = {k: v for k, v in _L0_xattn_all.items() if k in ('Wq', 'Wkv', 'Wo', 'g_in', 'g_out', 'null_kv')}
    del _L0_xattn_all

    def _L0_ffn_setup():
        import jax, jax.numpy as jnp
        import numpy as np
        HIDDEN = 128
        INNER = 512

        def _weight_quant(w):
            scale = 1.0 / jnp.clip(jnp.mean(jnp.abs(w)), 1e-05)
            wq = jnp.clip(jnp.round(w * scale), -1.0, 1.0) / scale
            return w + jax.lax.stop_gradient(wq - w)

        def _act_quant(x):
            scale = 127.0 / jnp.clip(jnp.max(jnp.abs(x), axis=-1, keepdims=True), 1e-05)
            xq = jnp.clip(jnp.round(x * scale), -128.0, 127.0) / scale
            return x + jax.lax.stop_gradient(xq - x)

        def _bitlinear(x, w):
            return jnp.einsum('bsi,oi->bso', _act_quant(x), _weight_quant(w))
        key = jax.random.key(seed)
        k0, k1, k2, k3 = jax.random.split(key, 4)
        x = jax.random.normal(k0, (4, 256, HIDDEN), dtype=jnp.float32)
        w_gate = jax.random.normal(k1, (INNER, HIDDEN), dtype=jnp.float32) / np.sqrt(HIDDEN)
        w_up = jax.random.normal(k2, (INNER, HIDDEN), dtype=jnp.float32) / np.sqrt(HIDDEN)
        w_down = jax.random.normal(k3, (HIDDEN, INNER), dtype=jnp.float32) / np.sqrt(INNER)
        return {'x': x, 'w_gate': w_gate, 'w_up': w_up, 'w_down': w_down}
    _L0_ffn_all = _L0_ffn_setup()
    _L0_ffn_in = {k: v for k, v in _L0_ffn_all.items() if k in ('w_gate', 'w_up', 'w_down')}
    del _L0_ffn_all
    return {'x': x, 'ctx_1024': ctx_1024, 'L0_xattn_Wq': _L0_xattn_in['Wq'], 'L0_xattn_Wkv': _L0_xattn_in['Wkv'], 'L0_xattn_Wo': _L0_xattn_in['Wo'], 'L0_xattn_g_in': _L0_xattn_in['g_in'], 'L0_xattn_g_out': _L0_xattn_in['g_out'], 'L0_xattn_null_kv': _L0_xattn_in['null_kv'], 'L0_ffn_w_gate': _L0_ffn_in['w_gate'], 'L0_ffn_w_up': _L0_ffn_in['w_up'], 'L0_ffn_w_down': _L0_ffn_in['w_down']}

def reference(x, ctx_1024, L0_xattn_Wq, L0_xattn_Wkv, L0_xattn_Wo, L0_xattn_g_in, L0_xattn_g_out, L0_xattn_null_kv, L0_ffn_w_gate, L0_ffn_w_up, L0_ffn_w_down):
    import jax
    import jax.numpy as jnp

    def _L0_xattn_ref(x, context, Wq, Wkv, Wo, g_in, g_out, null_kv):
        import jax, jax.numpy as jnp
        import numpy as np
        DIM = 128
        HEADS = 16
        DIM_HEAD = 64
        SCALE = DIM_HEAD ** (-0.5)
        EPS = 1e-05

        def stable_layernorm(x, g):
            x = x / jax.lax.stop_gradient(jnp.max(x, axis=-1, keepdims=True))
            mean = jnp.mean(x, axis=-1, keepdims=True)
            var = jnp.mean(jnp.square(x - mean), axis=-1, keepdims=True)
            return (x - mean) * jax.lax.rsqrt(var + EPS) * g
        b, n, _ = x.shape
        x = stable_layernorm(x, g_in)
        q = x @ Wq
        kv = context @ Wkv
        k, v = jnp.split(kv, 2, axis=-1)

        def to_heads(t):
            return t.reshape(b, t.shape[1], HEADS, DIM_HEAD).transpose(0, 2, 1, 3)
        q, k, v = (to_heads(q), to_heads(k), to_heads(v))
        nk = jnp.broadcast_to(null_kv[0], (b, HEADS, 1, DIM_HEAD))
        nv = jnp.broadcast_to(null_kv[1], (b, HEADS, 1, DIM_HEAD))
        k = jnp.concatenate([nk, k], axis=2)
        v = jnp.concatenate([nv, v], axis=2)
        q = q * SCALE
        sim = jnp.einsum('bhid,bhjd->bhij', q, k)
        attn = jax.nn.softmax(sim.astype(jnp.float32), axis=-1).astype(sim.dtype)
        out = jnp.einsum('bhij,bhjd->bhid', attn, v)
        out = out.transpose(0, 2, 1, 3).reshape(b, n, HEADS * DIM_HEAD)
        out = out @ Wo
        return stable_layernorm(out, g_out)

    def _L0_ffn_ref(x, w_gate, w_up, w_down):
        import jax, jax.numpy as jnp
        import numpy as np
        HIDDEN = 128
        INNER = 512

        def _weight_quant(w):
            scale = 1.0 / jnp.clip(jnp.mean(jnp.abs(w)), 1e-05)
            wq = jnp.clip(jnp.round(w * scale), -1.0, 1.0) / scale
            return w + jax.lax.stop_gradient(wq - w)

        def _act_quant(x):
            scale = 127.0 / jnp.clip(jnp.max(jnp.abs(x), axis=-1, keepdims=True), 1e-05)
            xq = jnp.clip(jnp.round(x * scale), -128.0, 127.0) / scale
            return x + jax.lax.stop_gradient(xq - x)

        def _bitlinear(x, w):
            return jnp.einsum('bsi,oi->bso', _act_quant(x), _weight_quant(w))
        gate = jax.nn.silu(_bitlinear(x, w_gate))
        up = _bitlinear(x, w_up)
        return _bitlinear(gate * up, w_down)
    x = x + _L0_xattn_ref(_layernorm(x, axis=-1), ctx_1024, L0_xattn_Wq, L0_xattn_Wkv, L0_xattn_Wo, L0_xattn_g_in, L0_xattn_g_out, L0_xattn_null_kv)
    x = x + _L0_ffn_ref(_layernorm(x, axis=-1), L0_ffn_w_gate, L0_ffn_w_up, L0_ffn_w_down)
    return x

_drawn_inputs = setup_inputs


def setup_inputs(seed=0):
    import zlib

    import numpy as np

    out = dict(_drawn_inputs(seed))
    spreads = {'L0_xattn_g_in': (1.0, 0.6), 'L0_xattn_g_out': (1.0, 0.2)}
    factors = {'L0_xattn_Wq': 3.82, 'L0_xattn_null_kv': 8.0}
    for name, (base, spread) in spreads.items():
        noise = np.random.default_rng([zlib.crc32(name.encode()), seed]).standard_normal(out[name].shape)
        drawn = base * np.exp(spread * noise) if base else spread * noise
        out[name] = jnp.asarray(drawn.astype(out[name].dtype))
    for name, factor in factors.items():
        out[name] = (out[name] * factor).astype(out[name].dtype)
    return out
```

```python
from contextlib import ExitStack

import concourse.bass as bass
from concourse import mybir

ALU = mybir.AluOpType
ACT = mybir.ActivationFunctionType
AX = mybir.AxisListType
F32 = mybir.dt.float32
F32R = mybir.dt.float32r
BF16 = mybir.dt.bfloat16

P = 128
B, N, D = 8, 56, 128
M = 1500
H, DH = 16, 64
INNER = H * DH
FF = 512
PAIRS = H // 2
QT = P // H
TILES = N // QT
ROWS = TILES * P
CH, CR = 12, 125
BANK, BANKS = 500, 3
CB = CH // BANKS
NB = 2
GROUPS = B // NB
GR = NB * N
SLOTS = NB * TILES
AHEAD = 4
TA = 4
CA = TA * P
CBW = ROWS - CA
EPS = 1e-5
ROUND = 1.5 * 2.0 ** 23
SCALE = DH ** -0.5


START = [("copy", "wqT0", ("probsT", 0)), ("copy", "wqT1", ("probsT", 1)),
         ("copy", "wkT0", ("probsT", 2)), ("copy", "wkT1", ("probsT", 0)),
         ("split", "ct0", ("scores", 0)), ("split", "ct1", ("scores", 1)), ("split", "ct2", ("scores", 2)),
         ("copy", "wf0", ("probsT", 1)), ("copy", "wf1", ("probsT", 2)),
         ("copy", "wf2", ("probsT", 0)), ("copy", "wf3", ("probsT", 1)),
         ("read", "wnk", ("attn", 0)), ("read", "xT", ("side", 0)),
         ("read", "n0", ("attn", 0)), ("read", "n1", ("side", 0)),
         ("split", "qk0", ("scores", 0)), ("split", "qk1", ("scores", 1)),
         ("split", "qk2", ("scores", 2)), ("split", "qk3", ("scores", 0))]
N_START = len(START)

PREP = [(2, 0, "ct0"), (3, 0, "ct1"), (4, 0, "ct2"), (10, 0, "ct0"), (12, 0, "ct1"), (12, 1, "ct2")]
FOLD = [(8, 0, "qk0"), (8, 1, "qk1"), (9, 0, "qk2"), (9, 1, "qk3")]
FINISH = [(6, 1, "u0"), (7, 0, "u1"), (7, 1, "o"), (10, 1, "xt"), (11, 0, "gate"), (11, 1, "up"),
          (13, 0, "ht"), (13, 1, "down")]
WEIGHTS = [(4, 1, "wsum"), (5, 1, "wgT"), (6, 1, "wuT"), (7, 1, "wdT"), (10, 1, "nvoT"), (11, 1, "nvo")]
SPLIT = ("qk0", "qk1", "qk2", "qk3", "ct0", "ct1", "ct2")
EARLY = ("ct0", "ct1", "ct2", "qk0", "qk1", "qk2", "qk3")
HEADS = 4
FINISH_OPS = 21


def steps_at(kind, u, place):
    steps = WEIGHTS if kind == "first" else FINISH
    if kind == "last":
        steps = steps + [x for x in PREP if x[0] < TILES]
    else:
        steps = steps + FOLD + PREP
    return [n for s, p, n in steps if (s, p) == (u, place)]


def steps_of(kind):
    return [n for u in range(SLOTS) for place in (0, 1) for n in steps_at(kind, u, place)]


N_FIRST, N_MIDDLE = len(steps_of("first")), len(steps_of("middle"))
N_SPLIT = len(PREP) + len(FOLD)


class Sides:

    def __init__(self, kind, g):
        self.n = self.split = 0
        self.base = 0 if kind == "first" else N_FIRST + N_MIDDLE * (g - 1)
        self.split_base = N_SPLIT * g
        if kind == "end":
            self.base = N_FIRST + N_MIDDLE * (GROUPS - 2) + len(steps_of("last"))

    def take(self, name):
        self.n += 1
        self.split += name in SPLIT
        return self.base + (self.n - 1), self.split_base + (self.split - 1)


def last_bank_at(v):
    return 2 * (v % AHEAD)


def wait(eng, semaphore, value):
    if isinstance(value, int) and value <= 0:
        return
    eng.wait_ge(semaphore, value)


def row(tensor, index):
    if isinstance(index, int):
        return tensor[0:GR, index, :]
    return tensor[0:GR, bass.ds(index, 1), :].rearrange("p a d -> p (a d)")


def build(nc, x, ctx, Wq, Wkv, Wo, g_in, g_out, null_kv, w_gate, w_up, w_down,
          identity, query_of, half_of, head_window, head_of, out):
    with ExitStack() as stack:
        def sb(name, shape, dt=F32):
            return stack.enter_context(nc.sbuf_tensor(name, shape, dt))

        def psum(name, shape, dt=F32):
            return stack.enter_context(nc.psum_tensor(name, shape, dt))

        def sem(name):
            return stack.enter_context(nc.semaphore(name))

        scores = psum("scores", [P, BANKS, 512])
        probsT = psum("probsT", [P, CH, P])
        attn = psum("attn", [P, 512])
        side = psum("side", [P, 512])
        side16 = side[:].bitcast(BF16)

        raw = sb("raw", [P, CH, D])
        ctx_hi = sb("ctx_hi", [P, 2, CH, D], F32R)
        ctx_lo = sb("ctx_lo", [P, 2, CH, D], F32R)
        ctxT_hi = sb("ctxT_hi", [P, 2, M], F32R)
        ctxT_lo = sb("ctxT_lo", [P, 2, M], F32R)
        qk_hi = sb("qk_hi", [P, 2, ROWS], F32R)
        qk_lo = sb("qk_lo", [P, 2, ROWS], F32R)
        qk_next = sb("qk_next", [P, ROWS])
        probs = sb("probs", [P, 2, M + 4])
        pT_hi = sb("pT_hi", [P, CH, ROWS], F32R)
        pT_lo = sb("pT_lo", [P, CH, ROWS], F32R)
        attnT = sb("attnT", [P, NB * ROWS])
        null_probs = sb("null_probs", [P, GROUPS * SLOTS])
        null_sel = sb("null_sel", [P, SLOTS, QT])
        fold = sb("fold", [P, H, D])
        wv = sb("wv", [P, INNER])
        wo = sb("wo", [P, PAIRS, D])
        ff_gate = sb("ff_gate", [P, FF], BF16)
        ff_up = sb("ff_up", [P, FF], BF16)
        ff_down = sb("ff_down", [P, FF], BF16)
        ff_q = sb("ff_q", [P, FF], BF16)
        work = sb("work", [P, 9 * D])
        uT = work[:, 0:PAIRS * GR].rearrange("p (h n) -> p h n", h=PAIRS)
        x2 = work[:, 0:D]
        hqT = work[:, D:3 * D].bitcast(BF16).rearrange("p (k n) -> p k n", n=P)
        yq = work[:, 3 * D:3 * D + D // 2].bitcast(BF16)
        yqT = work[:, 3 * D + D // 2:4 * D].bitcast(BF16)
        hidden = work[0:GR, 4 * D:8 * D]
        z = work[:, 8 * D:9 * D]
        ident = sb("ident", [P, P])
        ident16 = sb("ident16", [P, P], BF16)
        ones = sb("ones", [P, P])
        sel = sb("sel", [P, QT])
        null_v = sb("null_v", [P, 1])
        null_k = sb("null_k", [P, 1])
        halves = sb("halves", [P, 2])
        null_scores = sb("null_scores", [P, GROUPS * SLOTS])
        nvo = sb("nvo", [P, D])
        gin = sb("gin", [P, 1])
        gout = sb("gout", [P, D])
        xin = sb("xin", [P, GROUPS, D])
        xnT = sb("xnT", [P, GROUPS * GR])
        wq = probs[:, 0, 0:INNER]
        wk = probs[:, 1, 0:INNER]
        wqT = attnT[:, 0:INNER].rearrange("p (h d) -> p h d", h=PAIRS)
        wkT = work[:, 0:INNER].rearrange("p (h d) -> p h d", h=PAIRS)
        xw = attnT[0:GR, INNER:INNER + GROUPS * D].rearrange("p (g d) -> p g d", g=GROUPS)
        window = attnT[:, INNER + GROUPS * D:INNER + GROUPS * D + 240].rearrange("p (a b) -> p a b", b=15)
        raw_ffn = attnT[:, 0:3 * FF]
        wnk = qk_next[:, 0:H]
        head_rows = qk_next[0:H, H:H + P]
        n0 = qk_next[0:H, H + P:H + P + GROUPS * GR]
        stats = sb("stats", [P, GROUPS, 6])
        mv = sb("mv", [P, GROUPS, 2])
        ve = sb("ve", [P, GROUPS])
        rstd = sb("rstd", [P, GROUPS])
        mxs = sb("mxs", [P, GROUPS])
        minus_half = sb("minus_half", [P, GROUPS])
        part_max = sb("part_max", [P, 2, 2])
        neg_max = sb("neg_max", [P, 2])
        part_sum = sb("part_sum", [P, 2, BANKS])
        row_sum = sb("row_sum", [P, 2])
        inv_sum = sb("inv_sum", [P, 2])
        wabs = sb("wabs", [P, 3])
        wmean = sb("wmean", [P, 3])
        wscale = sb("wscale", [P, 3])
        result = sb("result", [P, D])
        f = sb("f", [P, 16])

        x_loaded = sem("x_loaded")
        small_loaded = sem("small_loaded")
        wk_loaded = sem("wk_loaded")
        wq_loaded = sem("wq_loaded")
        late_loaded = sem("late_loaded")
        ctx_loaded = sem("ctx_loaded")
        constants_set = sem("constants_set")
        start_step = sem("start_step")
        xn_ready = sem("xn_ready")
        start_filled = sem("start_filled")
        start_copied = sem("start_copied")
        start_read = sem("start_read")
        start_rounded = sem("start_rounded")
        start_split = sem("start_split")
        root_asked = sem("root_asked")
        root_done = sem("root_done")
        side_filled = sem("side_filled")
        side_drained = sem("side_drained")
        side_rounded = sem("side_rounded")
        side_tanh = sem("side_tanh")
        qk_stashed = sem("qk_stashed")
        qk_split = sem("qk_split")
        ctx_split = sem("ctx_split")
        scores_ready = sem("scores_ready")
        maxima_found = sem("maxima_found")
        neg_max_ready = sem("neg_max_ready")
        exp_done = sem("exp_done")
        sum_found = sem("sum_found")
        inv_ready = sem("inv_ready")
        probs_ready = sem("probs_ready")
        probsT_ready = sem("probsT_ready")
        pT_hi_ready = sem("pT_hi_ready")
        pT_lo_ready = sem("pT_lo_ready")
        attn_ready = sem("attn_ready")
        attn_drained = sem("attn_drained")
        finish_step = sem("finish_step")
        weights_step = sem("weights_step")
        weights_quantised = sem("weights_quantised")
        null_sel_ready = sem("null_sel_ready")
        rows_quantised = sem("rows_quantised")
        out_written = sem("out_written")

        x_rows = x.rearrange("b n d -> (b n) d")
        out_rows = out.rearrange("b n d -> (b n) d")
        ctx_v = ctx.rearrange("b (p c) d -> b p c d", c=CH)
        attn_by_head = attnT[:].rearrange("p (t e i h) -> p t e i h", e=2, i=QT, h=PAIRS)

        def by_head(a, e):
            return a.rearrange("p (t e i h) -> p e h t i", e=2, i=QT, h=PAIRS)[:, e]

        def bank_of(name):
            kind, k = name
            return {"probsT": probsT[:, 4 * k:4 * k + 4, :].rearrange("p c n -> p (c n)"),
                    "scores": scores[:, min(k, BANKS - 1), :], "attn": attn[:], "side": side[:]}[kind] \
                if kind != "probsT" else probsT[:].rearrange("p (k c) n -> p k (c n)", k=BANKS)[:, k]

        block = stack.enter_context(nc.Block())

        @block.sync
        def _(sp):
            sp.dma_start(xin[0:GR, :, :], x_rows.rearrange("(g p) d -> p g d", p=GR)).then_inc(x_loaded, 16)
            sp.dma_start(ident[:], identity).then_inc(small_loaded, 16)
            sp.dma_start(wq, Wq).then_inc(wq_loaded, 16)
            sp.dma_start(wk, Wkv[:, 0:INNER]).then_inc(wk_loaded, 16)
            sp.dma_start(raw[0:CR, :, :], ctx_v[0]).then_inc(ctx_loaded, 16)
            sp.dma_start(gin[:], g_in.rearrange("(d a) -> d a", a=1)).then_inc(small_loaded, 16)
            for e in range(2):
                sp.dma_start(null_k[e * DH:(e + 1) * DH, :], null_kv[0:1, :].rearrange("a d -> d a")
                             ).then_inc(small_loaded, 16)
            sp.dma_start(halves[:], half_of).then_inc(small_loaded, 16)
            sp.dma_start(head_rows, head_of).then_inc(small_loaded, 16)
            sp.dma_start(sel[:], query_of).then_inc(small_loaded, 16)

            def load(batch, transposed, count):
                sp.wait_ge(ctx_split, 2 * batch)
                sp.wait_ge(transposed, count)
                src = ctx_v[batch] if isinstance(batch, int) else \
                    ctx_v[bass.ds(batch, 1)].rearrange("a p c d -> p (a c) d")
                sp.dma_start(raw[0:CR, :, :], src).then_inc(ctx_loaded, 16)

            def store(group, kind):
                down = Sides(kind, group + 1).base + \
                    (steps_of(kind).index("down") if kind != "end" else len(FINISH) - 1)
                sp.wait_ge(side_drained, down + 1)
                dst = out_rows[GR * group:GR * group + GR, :] if isinstance(group, int) else \
                    out_rows[bass.ds(group * GR, GR), :]
                sp.dma_start(dst, result[0:GR, :]).then_inc(out_written, 16)

            sp.wait_ge(start_filled, N_START)
            load(1, start_rounded, 3)
            sp.dma_start(raw_ffn[:, 0:FF].rearrange("p (b d) -> p b d", d=D),
                         w_gate.rearrange("(b p) d -> p b d", p=P)).then_inc(late_loaded, 16)
            sp.dma_start(raw_ffn[:, FF:2 * FF].rearrange("p (b d) -> p b d", d=D),
                         w_up.rearrange("(b p) d -> p b d", p=P)).then_inc(late_loaded, 16)
            sp.dma_start(raw_ffn[:, 2 * FF:3 * FF], w_down).then_inc(late_loaded, 16)
            for e in range(2):
                sp.dma_start(null_v[e * DH:(e + 1) * DH, :], null_kv[1:2, :].rearrange("a d -> d a")
                             ).then_inc(late_loaded, 16)
            sp.dma_start(window, head_window).then_inc(late_loaded, 16)
            sp.dma_start(gout[0:GR, :], g_out.rearrange("(a d) -> a d", a=1).broadcast_to((GR, D))
                         ).then_inc(late_loaded, 16)
            sp.dma_start(wv[:], Wkv[:, INNER:2 * INNER]).then_inc(late_loaded, 16)
            sp.dma_start(wo[:], Wo.rearrange("(h p) d -> p h d", p=P)).then_inc(late_loaded, 16)
            load(2, side_rounded, 3)
            load(3, side_rounded, N_SPLIT)
            with sp.Fori(1, GROUPS - 1) as g:
                load(NB * g + 2, side_rounded, N_SPLIT * g + 3)
                store(g - 1, "middle")
                load(NB * g + 3, side_rounded, N_SPLIT * (g + 1))
            store(GROUPS - 2, "last")
            store(GROUPS - 1, "end")
            sp.wait_ge(out_written, 16 * GROUPS)

        LATE = 16 * 9
        SMALL = 16 * 7

        @block.gpsimd
        def _(pool):
            def root(cols, count):
                pool.wait_ge(root_asked, count)
                pool.tensor_tensor(rstd[0:GR, 0:cols], ve[0:GR, 0:cols], minus_half[0:GR, 0:cols],
                                   ALU.pow).then_inc(root_done, 1)

            def split_low(batch, par):
                pool.wait_ge(ctx_split, 2 * batch + 1)
                pool.tensor_tensor(ctx_lo[0:CR, par, :, :], raw[0:CR, :, :], ctx_hi[0:CR, par, :, :].bitcast(F32),
                                   ALU.subtract).then_inc(ctx_split, 1)

            def split_low_qk(g):
                pool.wait_ge(qk_split, 2 * g + 1)
                pool.tensor_tensor(qk_lo[:, 1, :], qk_next[:], qk_hi[:, 1, :].bitcast(F32), ALU.subtract
                                   ).then_inc(qk_split, 1)

            def normalise(g, u):
                s, par = SLOTS * g + u, u % 2
                pool.wait_ge(inv_ready, s + 1)
                inv = inv_sum[:, par:par + 1]
                null_out = null_probs[:, s:s + 1] if isinstance(s, int) else null_probs[:, bass.ds(s, 1)]
                pool.tensor_tensor(null_out, probs[:, par, M:M + 1], inv, ALU.mult).then_inc(probs_ready, 1)
                pool.tensor_scalar(probs[:, par, 0:M], probs[:, par, 0:M], inv, 1.0, ALU.mult, ALU.mult
                                   ).then_inc(probs_ready, 1)

            def group(kind, g):
                for u in range(SLOTS):
                    j, v = divmod(u, TILES)
                    if kind != "first" and u in (8, 9):
                        root(1, 2 + 2 * (g - 1) + (u - 8) + 1)
                    normalise(g, u)
                    if u == 1:
                        split_low_qk(g)
                    if v == TILES - 1 and not (kind == "last" and j == NB - 1):
                        split_low(NB * g + j + 1, (j + 1) % 2)

            pool.memset(minus_half[:], -0.5).then_inc(constants_set, 1)
            pool.memset(ones[:], 1.0).then_inc(constants_set, 1)
            pool.wait_ge(constants_set, 2)
            root(GROUPS, 1)
            root(GROUPS, 2)
            split_low(0, 0)
            group("first", 0)
            with pool.Fori(1, GROUPS - 1) as g:
                group("middle", g)
            group("last", GROUPS - 1)
            root(1, 2 + 2 * (GROUPS - 1) + 1)
            root(1, 2 + 2 * (GROUPS - 1) + 2)

        @block.scalar
        def _(act):
            def high_part(g, u):
                s = SLOTS * g + u - 2
                v, b = (u - 2) % TILES, NB * g + (u - 2) // TILES
                act.wait_ge(probsT_ready, s + 1)
                wait(act, attn_ready, 2 * (b - 1) + (1 if v < TA else 2))
                nc.scalar.copy(pT_hi[0:CR, :, v * P:(v + 1) * P], probsT[0:CR, :, :]).then_inc(pT_hi_ready, 1)

            def exps(g, u):
                s, par = SLOTS * g + u, u % 2
                act.wait_ge(neg_max_ready, s + 1)
                for k in range(BANKS):
                    n, at = (BANK + 1, last_bank_at(u % TILES)) if k == BANKS - 1 else (BANK, 0)
                    nc.scalar.activation(probs[:, par, k * BANK:k * BANK + n], scores[:, k, at:at + n], ACT.Exp,
                                         bias=neg_max[:, par:par + 1],
                                         accum_out=part_sum[:, par, k:k + 1]).then_inc(exp_done, 1)

            def round_qk(k, bank, rounded, stash):
                e, h = k // 2, HEADS * (k % 2)
                src = bank[:, 0:HEADS * GR].rearrange("p (h j t i) -> p h j t i", h=HEADS, j=NB, i=QT)
                nc.scalar.copy(by_head(qk_next[:], e)[:, h:h + HEADS], src[:, :, 1]).then_inc(qk_stashed, 1)
                nc.scalar.copy(by_head(qk_hi[:, 0, :], e)[:, h:h + HEADS], src[:, :, 0]).then_inc(rounded, 1)

            def side_step(name, sides, g, par):
                n, r = sides.take(name)
                if name in ("o", "wsum", "nvoT", "nvo", "up", "down"):
                    return
                act.wait_ge(side_filled, n + 1)
                if name in ("ct0", "ct1", "ct2"):
                    k = int(name[2])
                    nc.scalar.copy(ctxT_hi[:, par, k * BANK:(k + 1) * BANK], side[:, 0:BANK]
                                   ).then_inc(side_rounded, 1)
                elif name[0:2] == "qk":
                    if name == "qk0":
                        act.wait_ge(qk_split, 2 * g + 2)
                    round_qk(int(name[2]), side, side_rounded, None)
                elif name in ("u0", "u1"):
                    k = int(name[1])
                    nc.scalar.copy(uT[:, 4 * k:4 * k + 4, :], side[:, 0:4 * GR].rearrange("p (h n) -> p h n", h=4)
                                   ).then_inc(side_drained, 1)
                elif name == "xt":
                    nc.scalar.copy(yqT[:, 0:GR], side16[:, 0:GR]).then_inc(side_drained, 1)
                elif name == "gate":
                    nc.scalar.activation(hidden, side[0:GR, :], ACT.Tanh, scale=f[0:GR, 4:5]).then_inc(side_tanh, 1)
                elif name == "ht":
                    nc.scalar.copy(hqT[:, :, 0:GR], side16[:, 0:FF].rearrange("p (k n) -> p k n", n=P)[:, :, 0:GR]
                                   ).then_inc(side_drained, 1)
                elif name in ("wgT", "wuT", "wdT"):
                    dst = {"wgT": ff_gate, "wuT": ff_up, "wdT": ff_down}[name]
                    nc.scalar.copy(dst[:], side16[:, 0:FF]).then_inc(side_drained, 1)

            def drain_attn(g, u):
                j, v = divmod(u, TILES)
                b = NB * g + j - 1
                second = v == 5
                act.wait_ge(attn_ready, 2 * b + 1 + second)
                base = ROWS * ((j + 1) % 2)
                lo, hi = (CA, ROWS) if second else (0, CA)
                nc.scalar.copy(attnT[:, base + lo:base + hi], attn[:, 0:hi - lo]).then_inc(attn_drained, 1)

            def group(kind, g):
                sides = Sides(kind, g)
                for u in range(SLOTS):
                    j, v = divmod(u, TILES)
                    for name in steps_at(kind, u, 0):
                        side_step(name, sides, g, (j + 1) % 2)
                    if kind != "first" or u >= 2:
                        high_part(g, u)
                    for name in steps_at(kind, u, 1):
                        if name in EARLY:
                            side_step(name, sides, g, (j + 1) % 2)
                    exps(g, u)
                    for name in steps_at(kind, u, 1):
                        if name not in EARLY:
                            side_step(name, sides, g, (j + 1) % 2)
                    if v in (1, 5) and (kind != "first" or j == 1):
                        drain_attn(g, u)

            copied = [0]
            for n, (lane, name, bank) in enumerate(START):
                if lane == "read":
                    continue
                act.wait_ge(start_filled, n + 1)
                k = int(name[-1])
                if name[0:2] in ("wq", "wk"):
                    dst = wqT if name[1] == "q" else wkT
                    nc.scalar.copy(dst[:, 4 * k:4 * k + 4, :].rearrange("p h d -> p (h d)"), bank_of(bank)
                                   ).then_inc(start_copied, 1)
                elif name[0:2] == "wf":
                    nc.scalar.activation(fold[:, 4 * k:4 * k + 4, :].rearrange("p h d -> p (h d)"), bank_of(bank),
                                         ACT.Copy, scale=SCALE).then_inc(start_copied, 1)
                elif name[0:2] == "ct":
                    nc.scalar.copy(ctxT_hi[:, 0, k * BANK:(k + 1) * BANK], bank_of(bank)[:, 0:BANK]
                                   ).then_inc(start_rounded, 1)
                else:
                    if k == 0:
                        act.wait_ge(start_read, 4)
                    round_qk(k, bank_of(bank), start_rounded, None)
            group("first", 0)
            with act.Fori(1, GROUPS - 1) as g:
                group("middle", g)
            group("last", GROUPS - 1)
            for u in (SLOTS, SLOTS + 1):
                high_part(GROUPS - 1, u)
            drain_attn(GROUPS - 1, SLOTS + 1)
            drain_attn(GROUPS - 1, SLOTS + 5)
            sides = Sides("end", GROUPS)
            for _, _, name in FINISH:
                side_step(name, sides, GROUPS, 0)

        @block.vector
        def _(dve):
            def max_banks(g, u):
                s, par = SLOTS * g + u, u % 2
                dve.wait_ge(scores_ready, 2 * s + 1)
                dve.tensor_reduce(part_max[:, par, 0:1], scores[:, 0:2, 0:BANK], AX.XY, ALU.max
                                  ).then_inc(maxima_found, 1)

            def max_last(g, u):
                s, par = SLOTS * g + u, u % 2
                dve.wait_ge(scores_ready, 2 * s + 2)
                at = last_bank_at(u % TILES)
                dve.tensor_reduce(part_max[:, par, 1:2], scores[:, 2, at:at + BANK + 1], AX.X, ALU.max
                                  ).then_inc(maxima_found, 1)
                dve.wait_ge(maxima_found, 2 * s + 2)
                dve.tensor_reduce(neg_max[:, par:par + 1], part_max[:, par, :], AX.X, ALU.max, negate=True
                                  ).then_inc(neg_max_ready, 1)

            def invert_sums(g, u):
                s, par = SLOTS * g + u, u % 2
                dve.wait_ge(exp_done, BANKS * (s + 1))
                dve.tensor_reduce(row_sum[:, par:par + 1], part_sum[:, par, :], AX.X, ALU.add).then_inc(sum_found, 1)
                dve.wait_ge(sum_found, s + 1)
                dve.reciprocal(inv_sum[:, par:par + 1], row_sum[:, par:par + 1]).then_inc(inv_ready, 1)

            def low_part(g, u):
                s, v = SLOTS * g + u - 2, (u - 2) % TILES
                dve.wait_ge(pT_hi_ready, s + 1)
                cols = slice(v * P, (v + 1) * P)
                dve.tensor_tensor(pT_lo[0:CR, :, cols], probsT[0:CR, :, :], pT_hi[0:CR, :, cols].bitcast(F32),
                                  ALU.subtract).then_inc(pT_lo_ready, 1)

            def split_high(batch, par):
                dve.wait_ge(ctx_loaded, 16 * (batch + 1))
                wait(dve, attn_ready, 2 * (batch - 1))
                dve.tensor_copy(ctx_hi[0:CR, par, :, :], raw[0:CR, :, :]).then_inc(ctx_split, 1)

            fin = [0, 0]

            def chain(ins):
                fin[1] += 1
                ins.then_inc(finish_step, 1)
                dve.wait_ge(finish_step, FINISH_OPS * fin[0] + fin[1])

            def moments(src):
                chain(dve.bn_stats(stats[0:GR, 0, :], src))
                dve.memset(f[0:GR, 15:16], 0.0)
                chain(dve.bn_aggr(f[0:GR, 0:2], stats[0:GR, 0, :]))
                dve.tensor_scalar(ve[0:GR, 0:1], f[0:GR, 1:2], EPS, None, ALU.add).then_inc(root_asked, 1)

            def quantiser(src):
                chain(dve.tensor_reduce(f[0:GR, 2:3], src, AX.X, ALU.max, apply_absolute_value=True))
                chain(dve.tensor_scalar(f[0:GR, 7:8], f[0:GR, 2:3], EPS, 1.0 / 127.0, ALU.max, ALU.mult))
                chain(dve.reciprocal(f[0:GR, 3:4], f[0:GR, 7:8]))

            def finish_norm_out(sides_n):
                o = side[0:GR, 0:D]
                chain(dve.tensor_reduce(f[0:GR, 2:3], o, AX.X, ALU.max))
                chain(dve.reciprocal(f[0:GR, 3:4], f[0:GR, 2:3]))
                dve.tensor_scalar(z[0:GR, :], o, f[0:GR, 3:4], None, ALU.mult).then_inc(side_drained, 1)
                dve.wait_ge(side_drained, sides_n + 1)

            def finish_residual(grp):
                dve.wait_ge(root_done, 2 + 2 * grp + 1)
                chain(dve.tensor_scalar(z[0:GR, :], z[0:GR, :], f[0:GR, 0:1], rstd[0:GR, 0:1],
                                        ALU.subtract, ALU.mult))
                chain(dve.tensor_tensor(z[0:GR, :], z[0:GR, :], gout[0:GR, :], ALU.mult))
                chain(dve.tensor_tensor(x2[0:GR, :], z[0:GR, :], row(xin, grp), ALU.add))

            def finish_quantise(grp):
                dve.wait_ge(root_done, 2 + 2 * grp + 2)
                chain(dve.tensor_scalar(z[0:GR, :], x2[0:GR, :], f[0:GR, 0:1], rstd[0:GR, 0:1],
                                        ALU.subtract, ALU.mult))
                quantiser(z[0:GR, :])
                chain(dve.tensor_scalar(f[0:GR, 4:5], wmean[0:GR, 0:1], f[0:GR, 7:8], 0.5, ALU.mult, ALU.mult))
                chain(dve.tensor_scalar(f[0:GR, 5:6], wmean[0:GR, 1:2], f[0:GR, 7:8], f[0:GR, 4:5],
                                        ALU.mult, ALU.mult))

            def round_rows():
                chain(dve.tensor_scalar(z[0:GR, :], z[0:GR, :], f[0:GR, 3:4], ROUND, ALU.mult, ALU.add))
                dve.tensor_scalar(yq[0:GR, :], z[0:GR, :], ROUND, None, ALU.subtract).then_inc(rows_quantised, 1)

            def quantise_hidden():
                quantiser(hidden)
                chain(dve.tensor_scalar(f[0:GR, 8:9], wmean[0:GR, 2:3], f[0:GR, 7:8], None, ALU.mult))

            def finish_between(u, grp):
                if u == 8:
                    moments(z[0:GR, :])
                elif u == 9:
                    moments(x2[0:GR, :])
                elif u == 10:
                    round_rows()
                elif u == 12:
                    quantise_hidden()

            def finish_after(u, grp):
                if u == 8:
                    finish_residual(grp)
                elif u == 9:
                    finish_quantise(grp)
                elif u == 12:
                    round_hidden()

            def round_hidden():
                chain(dve.tensor_scalar(hidden, hidden, f[0:GR, 3:4], ROUND, ALU.mult, ALU.add))
                dve.tensor_scalar(ff_q[0:GR, :], hidden, ROUND, None, ALU.subtract).then_inc(rows_quantised, 1)

            def low_ctxT(k, par, bank, drained):
                cols = slice(k * BANK, (k + 1) * BANK)
                dve.tensor_tensor(ctxT_lo[:, par, cols], bank[:, 0:BANK], ctxT_hi[:, par, cols].bitcast(F32),
                                  ALU.subtract).then_inc(drained, 1)

            def low_qk(k, bank, drained):
                e, h = k // 2, HEADS * (k % 2)
                src = bank[:, 0:HEADS * GR].rearrange("p (h j t i) -> p h j t i", h=HEADS, j=NB, i=QT)
                dve.tensor_tensor(by_head(qk_lo[:, 0, :], e)[:, h:h + HEADS], src[:, :, 0],
                                  by_head(qk_hi[:, 0, :], e)[:, h:h + HEADS].bitcast(F32), ALU.subtract
                                  ).then_inc(drained, 1)

            def split_high_qk(g):
                dve.wait_ge(qk_stashed, 4 * (g + 1))
                dve.tensor_copy(qk_hi[:, 1, :], qk_next[:]).then_inc(qk_split, 1)

            def side_step(name, sides, g, par):
                n, r = sides.take(name)
                grp = g - 1
                if name in SPLIT:
                    dve.wait_ge(side_rounded, r + 1)
                    if name[0] == "c":
                        low_ctxT(int(name[2]), par, side, side_drained)
                    else:
                        dve.wait_ge(qk_stashed, 4 * (g + 1) + int(name[2]) + 1)
                        low_qk(int(name[2]), side, side_drained)
                elif name == "wsum":
                    dve.wait_ge(side_filled, n + 1)
                    dve.tensor_scalar(wmean[:], side[:, 0:3], 1.0 / (FF * D), EPS, ALU.mult, ALU.max
                                      ).then_inc(side_drained, 1)
                    dve.wait_ge(side_drained, n + 1)
                    dve.reciprocal(wscale[:], wmean[:]).then_inc(weights_step, 1)
                    quantise_weights(0, None)
                elif name in ("wgT", "wuT"):
                    dve.wait_ge(side_filled, n + 1)
                    quantise_weights(1 if name == "wgT" else 2, n)
                elif name in ("nvoT", "nvo"):
                    dve.wait_ge(side_filled, n + 1)
                    dve.tensor_copy(nvo[:], side[:, 0:D]).then_inc(side_drained, 1)
                elif name == "u0":
                    dve.wait_ge(probs_ready, 2 * SLOTS * g)
                    cols = null_probs[:, SLOTS * grp:SLOTS * g] if isinstance(grp, int) else \
                        null_probs[:, bass.ds(grp * SLOTS, SLOTS)]
                    dve.tensor_tensor(null_sel[:], cols.unsqueeze(2).broadcast_to((P, SLOTS, QT)),
                                      sel[:].unsqueeze(1).broadcast_to((P, SLOTS, QT)), ALU.mult
                                      ).then_inc(null_sel_ready, 1)
                elif name == "o":
                    fin[0], fin[1] = grp, 0
                    dve.wait_ge(side_filled, n + 1)
                    finish_norm_out(n)
                elif name == "gate":
                    dve.wait_ge(side_tanh, grp + 1)
                    dve.scalar_tensor_tensor(hidden, hidden, 1.0, side[0:GR, :], ALU.add, ALU.mult
                                             ).then_inc(side_drained, 1)
                elif name == "up":
                    dve.wait_ge(side_filled, n + 1)
                    dve.scalar_tensor_tensor(hidden, hidden, f[0:GR, 5:6], side[0:GR, :], ALU.mult, ALU.mult
                                             ).then_inc(side_drained, 1)
                    dve.wait_ge(side_drained, n + 1)
                elif name == "down":
                    dve.wait_ge(side_filled, n + 1)
                    wait(dve, out_written, 16 * grp)
                    dve.scalar_tensor_tensor(result[0:GR, :], side[0:GR, 0:D], f[0:GR, 8:9], x2[0:GR, :],
                                             ALU.mult, ALU.add).then_inc(side_drained, 1)

            wst = [1]

            def weights_chain(ins):
                wst[0] += 1
                ins.then_inc(weights_step, 1)

            def sum_weights():
                dve.wait_ge(late_loaded, LATE)
                for k in range(3):
                    dve.tensor_reduce(wabs[:, k:k + 1], raw_ffn[:, k * FF:(k + 1) * FF], AX.X, ALU.add,
                                      apply_absolute_value=True).then_inc(weights_quantised, 1)
                dve.tensor_scalar(window, window, null_v[:, 0:1], None, ALU.mult).then_inc(weights_quantised, 1)

            def quantise_weights(k, n):
                w = raw_ffn[:, k * FF:(k + 1) * FF]
                dve.wait_ge(weights_step, 1)
                weights_chain(dve.tensor_scalar(w, w, wscale[:, k:k + 1], ROUND, ALU.mult, ALU.add))
                dve.wait_ge(weights_step, wst[0])
                weights_chain(dve.tensor_scalar(w, w, ROUND, 1.0, ALU.subtract, ALU.min))
                dve.wait_ge(weights_step, wst[0])
                dve.tensor_scalar(ff_q[:], w, -1.0, None, ALU.max).then_inc(weights_quantised, 1)

            def group(kind, g):
                sides = Sides(kind, g)
                for u in range(SLOTS):
                    j, v = divmod(u, TILES)
                    max_banks(g, u)
                    for name in steps_at(kind, u, 0):
                        side_step(name, sides, g, (j + 1) % 2)
                    if kind != "first":
                        finish_between(u, g - 1)
                    max_last(g, u)
                    if kind != "first" or u >= 2:
                        low_part(g, u)
                    for name in steps_at(kind, u, 1):
                        if name in SPLIT:
                            side_step(name, sides, g, (j + 1) % 2)
                    invert_sums(g, u)
                    if u == 1:
                        split_high_qk(g)
                    if v == TILES - 1 and not (kind == "last" and j == NB - 1):
                        split_high(NB * g + j + 1, (j + 1) % 2)
                    if kind == "first" and u == 3:
                        sum_weights()
                    for name in steps_at(kind, u, 1):
                        if name not in SPLIT:
                            side_step(name, sides, g, (j + 1) % 2)
                    if kind != "first":
                        finish_after(u, g - 1)

            steps = [0]

            def start_chain(instructions):
                for ins in instructions:
                    steps[0] += 1
                    ins.then_inc(start_step, 1)
                dve.wait_ge(start_step, steps[0])

            def start_moments(src):
                start_chain([dve.bn_stats(stats[0:GR, k, :], src[0:GR, k, :]) for k in range(GROUPS)])
                start_chain([dve.bn_aggr(mv[0:GR, k, :], stats[0:GR, k, :]) for k in range(GROUPS)])
                dve.tensor_scalar(ve[0:GR, :], mv[0:GR, :, 1], EPS, None, ALU.add).then_inc(root_asked, 1)

            dve.wait_ge(x_loaded, 16)
            start_moments(xin)
            dve.wait_ge(root_done, 1)
            start_chain([dve.tensor_scalar(xw[:, k, :], xin[0:GR, k, :], mv[0:GR, k, 0:1], rstd[0:GR, k:k + 1],
                                           ALU.subtract, ALU.mult) for k in range(GROUPS)])
            start_chain([dve.tensor_reduce(mxs[0:GR, :], xw, AX.X, ALU.max)])
            start_chain([dve.reciprocal(ve[0:GR, :], mxs[0:GR, :])])
            start_chain([dve.tensor_scalar(xw[:, k, :], xw[:, k, :], ve[0:GR, k:k + 1], None, ALU.mult)
                         for k in range(GROUPS)])
            start_moments(xw)
            dve.wait_ge(root_done, 2)
            for k in range(GROUPS):
                dve.tensor_scalar(xw[:, k, :], xw[:, k, :], mv[0:GR, k, 0:1], rstd[0:GR, k:k + 1],
                                  ALU.subtract, ALU.mult).then_inc(xn_ready, 1)
            dve.wait_ge(small_loaded, SMALL)
            dve.tensor_copy(ident16[:], ident[:]).then_inc(xn_ready, 1)
            dve.tensor_scalar(halves[:], halves[:], null_k[:, 0:1], None, ALU.mult).then_inc(xn_ready, 1)
            for n, (lane, name, bank) in enumerate(START):
                src = bank_of(bank)
                if lane == "read":
                    dve.wait_ge(start_filled, n + 1)
                if name == "wnk":
                    dve.tensor_scalar(wnk, src[:, 0:H], SCALE, None, ALU.mult).then_inc(start_read, 1)
                elif name == "xT":
                    dve.tensor_scalar(xnT[:], src[:, 0:GROUPS * GR], gin[:, 0:1], None, ALU.mult
                                      ).then_inc(start_read, 1)
                elif name == "n0":
                    dve.tensor_copy(n0, src[0:H, 0:GROUPS * GR]).then_inc(start_read, 1)
                elif name == "n1":
                    slots, tmp = GROUPS * SLOTS, raw_ffn[:, 0:GROUPS * GR].rearrange("p (s i) -> p s i", i=QT)
                    dve.tensor_tensor(tmp, src[:, 0:GROUPS * GR].rearrange("p (s i) -> p s i", i=QT),
                                      sel[:].unsqueeze(1).broadcast_to((P, slots, QT)), ALU.mult
                                      ).then_inc(start_read, 1)
                    dve.wait_ge(start_read, 4)
                    dve.tensor_reduce(null_scores[:], tmp, AX.X, ALU.add).then_inc(start_read, 1)
                elif lane == "split":
                    k = int(name[-1])
                    dve.wait_ge(start_rounded, k + 1 if name[0] == "c" else 3 + k + 1)
                    if name[0] == "c":
                        low_ctxT(k, 0, src, start_split)
                    else:
                        dve.wait_ge(qk_stashed, k + 1)
                        low_qk(k, src, start_split)
            split_high(0, 0)
            group("first", 0)
            with dve.Fori(1, GROUPS - 1) as g:
                group("middle", g)
            group("last", GROUPS - 1)
            for u in (SLOTS, SLOTS + 1):
                low_part(GROUPS - 1, u)
            sides = Sides("end", GROUPS)
            for _, _, name in FINISH:
                if name == "xt":
                    moments(z[0:GR, :])
                    finish_residual(GROUPS - 1)
                    moments(x2[0:GR, :])
                    finish_quantise(GROUPS - 1)
                    round_rows()
                if name == "ht":
                    quantise_hidden()
                    round_hidden()
                side_step(name, sides, GROUPS, 0)
            assert fin[1] == FINISH_OPS, fin[1]

        @block.tensor
        def _(pe):
            def three_passes(out_ap, high, low, m_high, m_low, start, stop):
                nc.tensor.matmul(out_ap, high, m_high, start=start, stop=False)
                nc.tensor.matmul(out_ap, high, m_low, start=False, stop=False)
                return nc.tensor.matmul(out_ap, low, m_high, start=False, stop=stop)

            def score_banks(g, u, banks, prepared_at):
                j, v = divmod(u, TILES)
                s, par = SLOTS * g + u, j % 2
                if v == 0:
                    wait(pe, side_drained, prepared_at - (j == 0 and 0 in banks))
                    if j == 1 and 0 in banks:
                        pe.wait_ge(qk_split, 2 * g + 2)
                cols = slice(v * P, (v + 1) * P)
                for k in banks:
                    wait(pe, exp_done, BANKS * (s - 1) + k + 1)
                    keys = slice(k * BANK, (k + 1) * BANK)
                    at = last_bank_at(v) if k == BANKS - 1 else 0
                    if k == BANKS - 1 and at == 0:
                        n = min(AHEAD, TILES - v)
                        nc.tensor.matmul(scores[:, k, BANK:BANK + 2 * n - 1:2], ident[:],
                                         null_scores[:, s:s + n] if isinstance(s, int) else
                                         null_scores[:, bass.ds(s, n)], start=True, stop=True)
                    last = three_passes(scores[:, k, at:at + BANK], qk_hi[:, par, cols], qk_lo[:, par, cols],
                                        ctxT_hi[:, par, keys], ctxT_lo[:, par, keys], True, True)
                last.then_inc(scores_ready, 1)

            def transpose_probs(g, u):
                s, par = SLOTS * g + u - 2, u % 2
                pe.wait_ge(probs_ready, 2 * (s + 1))
                wait(pe, pT_lo_ready, s)
                for c in range(CH):
                    last = nc.tensor.transpose(probsT[0:CR, c, :], probs[:, par, c * CR:(c + 1) * CR], ident[:])
                last.then_inc(probsT_ready, 1)

            def probs_by_ctx(g, u):
                j, v = divmod(u, TILES)
                if v == TILES - 1:
                    b, jb, first, part, parts = NB * g + j, j, True, 0, 3
                elif v < 2:
                    b, jb, first, part, parts = NB * g + j - 1, j - 1, True, v + 1, 3
                else:
                    b, jb, first, part, parts = NB * g + j - 1, j - 1, False, v - 2, 4
                par = jb % 2
                lo, hi = (0, CA) if first else (CA, ROWS)
                if part == 0:
                    pe.wait_ge(pT_lo_ready, SLOTS * g + TILES * (j - (not first)) + (TA if first else TILES))
                    wait(pe, attn_drained, 2 * b + (not first))
                    pe.wait_ge(ctx_split, 2 * (b + 1))
                per = CH // parts
                for c in range(part * per, (part + 1) * per):
                    pairs = ((ctx_hi, pT_hi), (ctx_lo, pT_hi), (ctx_hi, pT_lo))
                    for i, (w, m) in enumerate(pairs):
                        last = nc.tensor.matmul(attn[:, 0:hi - lo], w[0:CR, par, c, :], m[0:CR, c, lo:hi],
                                                start=(c == 0 and i == 0), stop=(c == CH - 1 and i == 2))
                if part == parts - 1:
                    last.then_inc(attn_ready, 1)

            def transpose_ctx(k, bank):
                for i in range(CB):
                    last = nc.tensor.transpose(bank[:, i * CR:(i + 1) * CR], raw[0:CR, CB * k + i, :],
                                               ident[0:CR, 0:CR])
                return last

            def fold_queries(k, rows, bank):
                for i in range(HEADS):
                    last = nc.tensor.matmul(bank[:, i * GR:(i + 1) * GR], fold[:, HEADS * k + i, :], rows, start=True, stop=True)
                return last

            def side_step(name, sides, g, j):
                n, _ = sides.take(name)
                wait(pe, side_drained, n)
                if name in ("ct0", "ct1", "ct2"):
                    pe.wait_ge(ctx_loaded, 16 * (NB * g + j + 2))
                    last = transpose_ctx(int(name[2]), side)
                elif name[0:2] == "qk":
                    at = GR * (g + 1)
                    last = fold_queries(int(name[2]), xnT[:, at:at + GR] if isinstance(at, int) else
                                        xnT[:, bass.ds(at, GR)], side)
                elif name in ("u0", "u1"):
                    k = int(name[1])
                    if k == 0:
                        pe.wait_ge(attn_drained, 2 * NB * g)
                    for h in range(4 * k, 4 * k + 4):
                        for e in range(2):
                            last = nc.tensor.matmul(
                                side[e * DH:(e + 1) * DH, (h % 4) * GR:(h % 4 + 1) * GR],
                                wv[:, h * P + e * DH:h * P + (e + 1) * DH], attn_by_head[:, :, e, :, h],
                                start=True, stop=True)
                elif name == "o":
                    pe.wait_ge(null_sel_ready, g)
                    nc.tensor.matmul(side[0:GR, 0:D], null_sel[:].rearrange("p s i -> p (s i)"), nvo[:],
                                     start=True, stop=False)
                    for h in range(PAIRS):
                        last = nc.tensor.matmul(side[0:GR, 0:D], uT[:, h, :], wo[:, h, :],
                                                start=False, stop=(h == PAIRS - 1))
                elif name == "xt":
                    pe.wait_ge(rows_quantised, 2 * g - 1)
                    last = nc.tensor.transpose(side16[:, 0:GR], yq[0:GR, :], ident16[0:GR, 0:GR])
                elif name in ("gate", "up"):
                    w = ff_gate if name == "gate" else ff_up
                    last = nc.tensor.matmul(side[0:GR, :], yqT[:, 0:GR], w[:], start=True, stop=True)
                elif name == "ht":
                    pe.wait_ge(rows_quantised, 2 * g)
                    for k in range(FF // P):
                        last = nc.tensor.transpose(side16[:, k * P:k * P + GR], ff_q[0:GR, k * P:(k + 1) * P],
                                                   ident16[0:GR, 0:GR])
                elif name == "down":
                    for k in range(FF // P):
                        last = nc.tensor.matmul(side[0:GR, 0:D], hqT[:, k, 0:GR], ff_down[:, k * P:(k + 1) * P],
                                                start=(k == 0), stop=(k == FF // P - 1))
                elif name == "wsum":
                    pe.wait_ge(weights_quantised, 4)
                    last = nc.tensor.matmul(side[:, 0:3], ones[:], wabs[:], start=True, stop=True)
                elif name in ("wgT", "wuT", "wdT"):
                    pe.wait_ge(weights_quantised, 5 + ("wgT", "wuT", "wdT").index(name))
                    for k in range(FF // P):
                        last = nc.tensor.transpose(side16[:, k * P:(k + 1) * P], ff_q[:, k * P:(k + 1) * P],
                                                   ident16[:])
                elif name == "nvoT":
                    for h in range(PAIRS):
                        last = nc.tensor.matmul(side[:, 0:P], wo[:, h, :],
                                                window[:, :, PAIRS - 1 - h:2 * PAIRS - 1 - h],
                                                start=(h == 0), stop=(h == PAIRS - 1))
                elif name == "nvo":
                    last = nc.tensor.transpose(side[:, 0:D], nvo[:], ident[:])
                last.then_inc(side_filled, 1)

            def group(kind, g):
                sides = Sides(kind, g)
                prepared_at = sides.base
                for u in range(SLOTS):
                    j, v = divmod(u, TILES)
                    score_banks(g, u, (0, 1), prepared_at)
                    for name in steps_at(kind, u, 0):
                        side_step(name, sides, g, j)
                    if kind != "first" or u >= 2:
                        transpose_probs(g, u)
                    score_banks(g, u, (2,), prepared_at)
                    for name in steps_at(kind, u, 1):
                        side_step(name, sides, g, j)
                    if "ct2" in steps_at(kind, u, 0) + steps_at(kind, u, 1):
                        prepared_at = sides.base + sides.n
                    if kind != "first" or u >= TILES - 1:
                        probs_by_ctx(g, u)

            lanes = {"copy": 0, "read": 0, "split": 0}
            for n, (lane, name, bank) in enumerate(START):
                done, banks = {"copy": (start_copied, 3), "read": (start_read, 2), "split": (start_split, 3)}[lane]
                wait(pe, done, lanes[lane] - banks + 1)
                lanes[lane] += 1
                out_bank = bank_of(bank)
                k = int(name[-1]) if name[-1].isdigit() else 0
                if name[0:3] in ("wqT", "wkT"):
                    w, loaded = (wq, wq_loaded) if name[1] == "q" else (wk, wk_loaded)
                    pe.wait_ge(loaded, 16)
                    if n == 0:
                        pe.wait_ge(small_loaded, SMALL)
                    for i in range(4):
                        c = (4 * k + i) * P
                        last = nc.tensor.transpose(out_bank[:, i * P:(i + 1) * P], w[:, c:c + P], ident[:])
                elif name[0:2] == "wf":
                    if k == 0:
                        pe.wait_ge(start_copied, 4)
                    for i in range(4):
                        e, hp = divmod(4 * k + i, PAIRS)
                        half = slice(e * DH, (e + 1) * DH)
                        last = nc.tensor.matmul(out_bank[:, i * P:(i + 1) * P], wqT[half, hp, :], wkT[half, hp, :],
                                                start=True, stop=True)
                elif name[0:2] == "ct":
                    pe.wait_ge(ctx_loaded, 16)
                    last = transpose_ctx(k, out_bank)
                elif name == "wnk":
                    pe.wait_ge(xn_ready, GROUPS + 2)
                    pe.wait_ge(start_copied, 2)
                    for hp in range(PAIRS):
                        last = nc.tensor.matmul(out_bank[:, 2 * hp:2 * hp + 2], wqT[:, hp, :], halves[:],
                                                start=True, stop=True)
                elif name == "xT":
                    for i in range(GROUPS):
                        last = nc.tensor.transpose(out_bank[:, i * GR:(i + 1) * GR], xw[:, i, :],
                                                   ident[0:GR, 0:GR])
                elif name == "n0":
                    pe.wait_ge(start_read, 2)
                    last = nc.tensor.matmul(out_bank[0:H, 0:GROUPS * GR], wnk, xnT[:], start=True, stop=True)
                elif name == "n1":
                    pe.wait_ge(start_read, 3)
                    last = nc.tensor.matmul(out_bank[:, 0:GROUPS * GR], head_rows, n0, start=True, stop=True)
                else:
                    if k == 0:
                        pe.wait_ge(start_copied, 8)
                    last = fold_queries(k, xnT[:, 0:GR], out_bank)
                last.then_inc(start_filled, 1)
            pe.wait_ge(start_split, 7)
            pe.wait_ge(start_read, 5)
            pe.wait_ge(constants_set, 2)
            group("first", 0)
            with pe.Fori(1, GROUPS - 1) as g:
                group("middle", g)
            group("last", GROUPS - 1)
            for u in range(SLOTS, SLOTS + TILES - 1):
                if u < SLOTS + 2:
                    transpose_probs(GROUPS - 1, u)
                probs_by_ctx(GROUPS - 1, u)
            sides = Sides("end", GROUPS)
            for _, _, name in FINISH:
                side_step(name, sides, GROUPS, 0)


_INS = ["x", "ctx_1024", "L0_xattn_Wq", "L0_xattn_Wkv", "L0_xattn_Wo", "L0_xattn_g_in", "L0_xattn_g_out",
        "L0_xattn_null_kv", "L0_ffn_w_gate", "L0_ffn_w_up", "L0_ffn_w_down"]


def kernel(**inputs):
    import numpy as _np
    import concourse.bacc as _bacc
    from concourse import mybir as _mybir
    from concourse.bass_utils import run_bass_kernel_spmd as _run

    nc = _bacc.Bacc("TRN2", target_bir_lowering=False, num_devices=1)
    arrays = {n: _np.ascontiguousarray(inputs[n]) for n in _INS}
    r = _np.arange(P)
    arrays["identity"] = _np.eye(P, dtype=_np.float32)
    arrays["query_of"] = (((r % DH) // PAIRS)[:, None] == _np.arange(QT)[None, :]).astype(_np.float32)
    window = _np.zeros((P, 2, QT, 15), _np.float32)
    window[0:DH, 0, :, PAIRS - 1] = 1.0
    window[DH:P, 1, :, PAIRS - 1] = 1.0
    arrays["half_of"] = (r[:, None] // DH == _np.arange(2)[None, :]).astype(_np.float32)
    arrays["head_window"] = window.reshape(P, 16, 15)
    arrays["head_of"] = (_np.arange(H)[:, None] == (2 * (r % PAIRS) + r // DH)[None, :]).astype(_np.float32)
    args = [nc.dram_tensor(f"in_{n}_dram", a.shape, _mybir.dt.from_np(a.dtype), kind="ExternalInput").ap()
            for n, a in arrays.items()]
    out = nc.dram_tensor("out_0_dram", (B, N, D), _mybir.dt.float32, kind="ExternalOutput").ap()
    build(nc, *args, out)
    got = _run(nc, [{f"in_{n}_dram": a for n, a in arrays.items()}], core_ids=[0])
    return got.results[0]["out_0_dram"]
```

```python
from contextlib import ExitStack

import concourse.bass as bass
from concourse import mybir

ALU = mybir.AluOpType
ACT = mybir.ActivationFunctionType
AX = mybir.AxisListType
F32 = mybir.dt.float32
F32R = mybir.dt.float32r
BF16 = mybir.dt.bfloat16

P = 128
B, N, D = 8, 56, 128
M = 1500
H, DH = 16, 64
INNER = H * DH
FF = 512
PAIRS = H // 2
QT = P // H
TILES = N // QT
ROWS = TILES * P
CH, CR = 12, 125
BANK, BANKS = 500, 3
CB = CH // BANKS
NB = 2
GROUPS = B // NB
GR = NB * N
SLOTS = NB * TILES
AHEAD = 4
TA, TA_LAST = 3, 4
LATE_C = 8
EPS = 1e-5
ROUND = 1.5 * 2.0 ** 23
SCALE = DH ** -0.5


START = [("copy", "wqT0", ("probsT", 0)), ("copy", "wqT1", ("probsT", 1)),
         ("copy", "wkT0", ("probsT", 2)), ("copy", "wkT1", ("probsT", 0)),
         ("copy", "wf0", ("probsT", 1)), ("copy", "wf1", ("probsT", 2)),
         ("copy", "wf2", ("probsT", 0)), ("copy", "wf3", ("probsT", 1)),
         ("split", "ct0", ("scores", 0)), ("split", "ct1", ("scores", 1)), ("split", "ct2", ("scores", 2)),
         ("read", "xT", ("attn", 0)), ("read", "wnk", ("side", 0)),
         ("split", "qk0", ("scores", 0)), ("read", "n0", ("attn", 0)),
         ("split", "qk1", ("scores", 1)), ("read", "n1", ("side", 0)),
         ("split", "qk2", ("scores", 2)), ("split", "qk3", ("scores", 0))]
VECTOR_ORDER = ("xT", "ct0", "ct1", "wnk", "ct2", "qk0", "n0", "qk1", "n1", "qk2", "qk3")
WARM = 12
N_START = len(START)

PREP = [(2, 0, "ct0"), (3, 0, "ct1"), (4, 0, "ct2"), (10, 0, "ct0"), (12, 0, "ct1"), (12, 1, "ct2")]
FOLD = [(8, 0, "qk0"), (8, 1, "qk1"), (9, 0, "qk2"), (9, 1, "qk3")]
FINISH = [(6, 1, "u0"), (7, 0, "u1"), (7, 1, "o"), (10, 1, "xt"), (11, 0, "gate"), (11, 1, "up"),
          (13, 0, "ht"), (13, 1, "down")]
WEIGHTS = [(4, 1, "wsum"), (5, 1, "wgT"), (6, 1, "wuT"), (7, 1, "wdT"), (10, 1, "nvoT"), (11, 0, "nvo")]
SPLIT = ("qk0", "qk1", "qk2", "qk3", "ct0", "ct1", "ct2")
EARLY = ("ct0", "ct1", "ct2", "qk0", "qk1", "qk2", "qk3", "xt")
HEADS = 4
POOL_OPS = 4
FINISH_OPS = 15


def steps_at(kind, u, place):
    steps = WEIGHTS if kind == "first" else FINISH
    if kind == "last":
        steps = steps + [x for x in PREP if x[0] < TILES]
    else:
        steps = steps + FOLD + PREP
    return [n for s, p, n in steps if (s, p) == (u, place)]


def steps_of(kind):
    return [n for u in range(SLOTS) for place in (0, 1) for n in steps_at(kind, u, place)]


N_FIRST, N_MIDDLE = len(steps_of("first")), len(steps_of("middle"))
N_SPLIT = len(PREP) + len(FOLD)


class Sides:

    def __init__(self, kind, g):
        self.n = self.split = 0
        self.base = 0 if kind == "first" else N_FIRST + N_MIDDLE * (g - 1)
        self.split_base = N_SPLIT * g
        if kind == "end":
            self.base = N_FIRST + N_MIDDLE * (GROUPS - 2) + len(steps_of("last"))

    def take(self, name):
        self.n += 1
        self.split += name in SPLIT
        return self.base + (self.n - 1), self.split_base + (self.split - 1)


def part_columns(kind, j, second):
    at = P * (TA_LAST if kind == "last" and j == NB - 1 else TA)
    return (at, ROWS) if second else (0, at)


def last_bank_at(v):
    return 2 * (v % AHEAD)


def wait(eng, semaphore, value):
    if isinstance(value, int) and value <= 0:
        return
    eng.wait_ge(semaphore, value)


def row(tensor, index):
    if isinstance(index, int):
        return tensor[0:GR, index, :]
    return tensor[0:GR, bass.ds(index, 1), :].rearrange("p a d -> p (a d)")


def build(nc, x, ctx, Wq, Wkv, Wo, g_in, g_out, null_kv, w_gate, w_up, w_down,
          identity, query_of, half_of, head_window, head_of, out):
    with ExitStack() as stack:
        def sb(name, shape, dt=F32):
            return stack.enter_context(nc.sbuf_tensor(name, shape, dt))

        def psum(name, shape, dt=F32):
            return stack.enter_context(nc.psum_tensor(name, shape, dt))

        def sem(name):
            return stack.enter_context(nc.semaphore(name))

        scores = psum("scores", [P, BANKS, 512])
        probsT = psum("probsT", [P, CH, P])
        attn = psum("attn", [P, 512])
        side = psum("side", [P, 512])
        side16 = side[:].bitcast(BF16)

        raw = sb("raw", [P, CH, D])
        ctx_hi = sb("ctx_hi", [P, 2, CH, D], F32R)
        ctx_lo = sb("ctx_lo", [P, 2, CH, D], F32R)
        ctxT_hi = sb("ctxT_hi", [P, 2, M], F32R)
        ctxT_lo = sb("ctxT_lo", [P, 2, M], F32R)
        qk_hi = sb("qk_hi", [P, 2, ROWS], F32R)
        qk_lo = sb("qk_lo", [P, 2, ROWS], F32R)
        qk_next = sb("qk_next", [P, ROWS])
        probs = sb("probs", [P, 2, M + 4])
        pT_hi = sb("pT_hi", [P, CH, ROWS], F32R)
        pT_lo = sb("pT_lo", [P, CH, ROWS], F32R)
        attnT = sb("attnT", [P, NB * ROWS])
        null_probs = sb("null_probs", [P, GROUPS * SLOTS])
        null_sel = sb("null_sel", [P, SLOTS, QT])
        fold = sb("fold", [P, H, D])
        wv = sb("wv", [P, INNER])
        wo = sb("wo", [P, PAIRS, D])
        ff_gate = sb("ff_gate", [P, FF], BF16)
        ff_up = sb("ff_up", [P, FF], BF16)
        ff_down = sb("ff_down", [P, FF], BF16)
        ff_q = sb("ff_q", [P, FF], BF16)
        work = sb("work", [P, 9 * D])
        uT = work[:, 0:PAIRS * GR].rearrange("p (h n) -> p h n", h=PAIRS)
        x2 = work[:, 0:D]
        hqT = work[:, D:3 * D].bitcast(BF16).rearrange("p (k n) -> p k n", n=P)
        yq = work[:, 3 * D:3 * D + D // 2].bitcast(BF16)
        yqT = work[:, 3 * D + D // 2:4 * D].bitcast(BF16)
        hidden = work[0:GR, 4 * D:8 * D]
        z = work[:, 8 * D:9 * D]
        ident = sb("ident", [P, P])
        ident16 = sb("ident16", [P, P], BF16)
        ones = sb("ones", [P, P])
        sel = sb("sel", [P, QT])
        null_v = sb("null_v", [P, 1])
        null_k = sb("null_k", [P, 1])
        halves = sb("halves", [P, 2])
        null_scores = sb("null_scores", [P, GROUPS * SLOTS])
        nvo = sb("nvo", [P, D])
        gin = sb("gin", [P, 1])
        gout = sb("gout", [P, D])
        result = sb("result", [P, D])
        xin = sb("xin", [P, GROUPS, D])
        xnT = sb("xnT", [P, GROUPS * GR])
        wq = probs[:, 0, 0:INNER]
        wk = probs[:, 1, 0:INNER]
        wqT = attnT[:, 0:INNER].rearrange("p (h d) -> p h d", h=PAIRS)
        wkT = work[:, 0:INNER].rearrange("p (h d) -> p h d", h=PAIRS)
        xw = attnT[0:GR, INNER:INNER + GROUPS * D].rearrange("p (g d) -> p g d", g=GROUPS)
        window = attnT[:, INNER + GROUPS * D:INNER + GROUPS * D + 240].rearrange("p (a b) -> p a b", b=15)
        raw_ffn = attnT[:, 0:3 * FF]
        wnk = result[:, 0:H]
        head_rows = gout[0:H, :]
        n0 = probs[0:H, 0, INNER:INNER + GROUPS * GR]
        null_rows = probs[:, 1, INNER:INNER + GROUPS * GR].rearrange("p (s i) -> p s i", i=QT)
        stats = sb("stats", [P, GROUPS, 6])
        mv = sb("mv", [P, GROUPS, 2])
        ve = sb("ve", [P, GROUPS])
        rstd = sb("rstd", [P, GROUPS])
        mxs = sb("mxs", [P, GROUPS])
        minus_half = sb("minus_half", [P, GROUPS])
        part_max = sb("part_max", [P, 2, 2])
        neg_max = sb("neg_max", [P, 2])
        part_sum = sb("part_sum", [P, 2, BANKS])
        row_sum = sb("row_sum", [P, 2])
        inv_sum = sb("inv_sum", [P, 2])
        wabs = sb("wabs", [P, 3])
        wmean = sb("wmean", [P, 3])
        wscale = sb("wscale", [P, 3])
        f = sb("f", [P, 16])

        x_loaded = sem("x_loaded")
        ident_loaded = sem("ident_loaded")
        small_loaded = sem("small_loaded")
        wk_loaded = sem("wk_loaded")
        wq_loaded = sem("wq_loaded")
        late_loaded = sem("late_loaded")
        ctx_loaded = sem("ctx_loaded")
        constants_set = sem("constants_set")
        start_step = sem("start_step")
        xn_ready = sem("xn_ready")
        start_filled = sem("start_filled")
        start_copied = sem("start_copied")
        start_read = sem("start_read")
        start_rounded = sem("start_rounded")
        start_split = sem("start_split")
        root_asked = sem("root_asked")
        root_done = sem("root_done")
        side_filled = sem("side_filled")
        side_drained = sem("side_drained")
        side_rounded = sem("side_rounded")
        side_tanh = sem("side_tanh")
        qk_stashed = sem("qk_stashed")
        qk_split = sem("qk_split")
        ctx_split = sem("ctx_split")
        scores_ready = sem("scores_ready")
        maxima_found = sem("maxima_found")
        neg_max_ready = sem("neg_max_ready")
        exp_done = sem("exp_done")
        sum_found = sem("sum_found")
        inv_ready = sem("inv_ready")
        probs_ready = sem("probs_ready")
        late_hi_ready = sem("late_hi_ready")
        late_lo_ready = sem("late_lo_ready")
        probsT_ready = sem("probsT_ready")
        pT_hi_ready = sem("pT_hi_ready")
        pT_lo_ready = sem("pT_lo_ready")
        attn_ready = sem("attn_ready")
        attn_drained = sem("attn_drained")
        finish_step = sem("finish_step")
        weights_step = sem("weights_step")
        weights_quantised = sem("weights_quantised")
        rounding_asked = sem("rounding_asked")
        pool_step = sem("pool_step")
        scales_ready = sem("scales_ready")
        null_sel_ready = sem("null_sel_ready")
        rows_quantised = sem("rows_quantised")
        out_written = sem("out_written")

        x_rows = x.rearrange("b n d -> (b n) d")
        out_rows = out.rearrange("b n d -> (b n) d")
        ctx_v = ctx.rearrange("b (p c) d -> b p c d", c=CH)
        attn_by_head = attnT[:].rearrange("p (t e i h) -> p t e i h", e=2, i=QT, h=PAIRS)

        def by_head(a, e):
            return a.rearrange("p (t e i h) -> p e h t i", e=2, i=QT, h=PAIRS)[:, e]

        def bank_of(name):
            kind, k = name
            return {"probsT": probsT[:, 4 * k:4 * k + 4, :].rearrange("p c n -> p (c n)"),
                    "scores": scores[:, min(k, BANKS - 1), :], "attn": attn[:], "side": side[:]}[kind] \
                if kind != "probsT" else probsT[:].rearrange("p (k c) n -> p k (c n)", k=BANKS)[:, k]

        block = stack.enter_context(nc.Block())

        @block.sync
        def _(sp):
            sp.dma_start(xin[0:GR, :, :], x_rows.rearrange("(g p) d -> p g d", p=GR)).then_inc(x_loaded, 16)
            sp.dma_start(ident[:], identity).then_inc(ident_loaded, 16)
            sp.dma_start(wq, Wq).then_inc(wq_loaded, 16)
            sp.dma_start(wk, Wkv[:, 0:INNER]).then_inc(wk_loaded, 16)
            sp.dma_start(raw[0:CR, :, :], ctx_v[0]).then_inc(ctx_loaded, 16)
            sp.dma_start(gin[:], g_in.rearrange("(d a) -> d a", a=1)).then_inc(small_loaded, 16)
            for e in range(2):
                sp.dma_start(null_k[e * DH:(e + 1) * DH, :], null_kv[0:1, :].rearrange("a d -> d a")
                             ).then_inc(small_loaded, 16)
            sp.dma_start(halves[:], half_of).then_inc(small_loaded, 16)
            sp.dma_start(head_rows, head_of).then_inc(small_loaded, 16)
            sp.dma_start(sel[:], query_of).then_inc(small_loaded, 16)

            def load(batch, transposed, count):
                sp.wait_ge(ctx_split, 2 * batch)
                sp.wait_ge(transposed, count)
                src = ctx_v[batch] if isinstance(batch, int) else \
                    ctx_v[bass.ds(batch, 1)].rearrange("a p c d -> p (a c) d")
                sp.dma_start(raw[0:CR, :, :], src).then_inc(ctx_loaded, 16)

            def store(group, kind):
                down = Sides(kind, group + 1).base + \
                    (steps_of(kind).index("down") if kind != "end" else len(FINISH) - 1)
                sp.wait_ge(side_drained, down + 1)
                dst = out_rows[GR * group:GR * group + GR, :] if isinstance(group, int) else \
                    out_rows[bass.ds(group * GR, GR), :]
                sp.dma_start(dst, result[0:GR, :]).then_inc(out_written, 16)

            load(1, start_rounded, 3)
            sp.wait_ge(start_filled, N_START)
            sp.wait_ge(start_read, 5)
            sp.dma_start(raw_ffn[:, 0:FF].rearrange("p (b d) -> p b d", d=D),
                         w_gate.rearrange("(b p) d -> p b d", p=P)).then_inc(late_loaded, 16)
            sp.dma_start(raw_ffn[:, FF:2 * FF].rearrange("p (b d) -> p b d", d=D),
                         w_up.rearrange("(b p) d -> p b d", p=P)).then_inc(late_loaded, 16)
            sp.dma_start(raw_ffn[:, 2 * FF:3 * FF], w_down).then_inc(late_loaded, 16)
            for e in range(2):
                sp.dma_start(null_v[e * DH:(e + 1) * DH, :], null_kv[1:2, :].rearrange("a d -> d a")
                             ).then_inc(late_loaded, 16)
            sp.dma_start(window, head_window).then_inc(late_loaded, 16)
            sp.dma_start(gout[0:GR, :], g_out.rearrange("(a d) -> a d", a=1).broadcast_to((GR, D))
                         ).then_inc(late_loaded, 16)
            sp.dma_start(wv[:], Wkv[:, INNER:2 * INNER]).then_inc(late_loaded, 16)
            sp.dma_start(wo[:], Wo.rearrange("(h p) d -> p h d", p=P)).then_inc(late_loaded, 16)
            load(2, side_rounded, 3)
            load(3, side_rounded, N_SPLIT)
            with sp.Fori(1, GROUPS - 1) as g:
                load(NB * g + 2, side_rounded, N_SPLIT * g + 3)
                store(g - 1, "middle")
                load(NB * g + 3, side_rounded, N_SPLIT * (g + 1))
            store(GROUPS - 2, "last")
            store(GROUPS - 1, "end")
            sp.wait_ge(out_written, 16 * GROUPS)

        LATE = 16 * 9
        SMALL = 16 * 6

        @block.gpsimd
        def _(pool):
            def root(cols, count):
                pool.wait_ge(root_asked, count)
                pool.tensor_tensor(rstd[0:GR, 0:cols], ve[0:GR, 0:cols], minus_half[0:GR, 0:cols],
                                   ALU.pow).then_inc(root_done, 1)

            def split_low(batch, par):
                pool.wait_ge(ctx_split, 2 * batch + 1)
                pool.tensor_tensor(ctx_lo[0:CR, par, :, :], raw[0:CR, :, :], ctx_hi[0:CR, par, :, :].bitcast(F32),
                                   ALU.subtract).then_inc(ctx_split, 1)

            def split_low_qk(g):
                pool.wait_ge(qk_split, 2 * g + 1)
                pool.tensor_tensor(qk_lo[:, 1, :], qk_next[:], qk_hi[:, 1, :].bitcast(F32), ALU.subtract
                                   ).then_inc(qk_split, 1)

            def normalise(g, u):
                s, par = SLOTS * g + u, u % 2
                pool.wait_ge(inv_ready, s + 1)
                inv = inv_sum[:, par:par + 1]
                null_out = null_probs[:, s:s + 1] if isinstance(s, int) else null_probs[:, bass.ds(s, 1)]
                pool.tensor_tensor(null_out, probs[:, par, M:M + 1], inv, ALU.mult).then_inc(probs_ready, 1)
                pool.tensor_scalar(probs[:, par, 0:M], probs[:, par, 0:M], inv, 1.0, ALU.mult, ALU.mult
                                   ).then_inc(probs_ready, 1)

            def group(kind, g):
                for u in range(SLOTS):
                    j, v = divmod(u, TILES)
                    if kind != "first" and u in (8, 9):
                        root(1, 2 + 2 * (g - 1) + (u - 8) + 1)
                    if kind != "first" and u == 9:
                        round_rows(g - 1)
                    if kind != "first" and u == 12:
                        round_hidden(g - 1)
                    normalise(g, u)
                    if kind != "first" and u == 9:
                        scales(g - 1)
                    if u == 1:
                        split_low_qk(g)
                    if v == TILES - 1 and not (kind == "last" and j == NB - 1):
                        split_low(NB * g + j + 1, (j + 1) % 2)

            def carry():
                pool.tensor_tensor(f[0:GR, 14:15], minus_half[0:GR, 0:1], minus_half[0:GR, 0:1], ALU.mult)

            def round_rows(grp):
                pool.wait_ge(rounding_asked, 2 * grp + 1)
                carry()
                pool.tensor_scalar(z[0:GR, :], z[0:GR, :], rstd[0:GR, 0:1], f[0:GR, 3:4], ALU.mult, ALU.mult
                                   ).then_inc(pool_step, 1)
                pool.wait_ge(pool_step, POOL_OPS * grp + 1)
                carry()
                pool.tensor_scalar(z[0:GR, :], z[0:GR, :], ROUND, 1.0, ALU.add, ALU.mult).then_inc(pool_step, 1)
                pool.wait_ge(pool_step, POOL_OPS * grp + 2)
                carry()
                pool.tensor_scalar(yq[0:GR, :], z[0:GR, :], ROUND, 1.0, ALU.subtract, ALU.mult
                                   ).then_inc(rows_quantised, 1)

            def scales(grp):
                pool.tensor_scalar(f[0:GR, 4:5], wmean[0:GR, 0:1], f[0:GR, 7:8], 0.5, ALU.mult, ALU.mult
                                   ).then_inc(pool_step, 1)
                pool.wait_ge(pool_step, POOL_OPS * grp + 3)
                carry()
                pool.tensor_scalar(f[0:GR, 5:6], wmean[0:GR, 1:2], f[0:GR, 7:8], f[0:GR, 4:5],
                                   ALU.mult, ALU.mult).then_inc(scales_ready, 1)

            def round_hidden(grp):
                pool.wait_ge(rounding_asked, 2 * grp + 2)
                carry()
                pool.tensor_scalar(hidden, hidden, f[0:GR, 3:4], ROUND, ALU.mult, ALU.add).then_inc(pool_step, 1)
                pool.wait_ge(pool_step, POOL_OPS * grp + 4)
                carry()
                pool.tensor_scalar(ff_q[0:GR, :], hidden, ROUND, 1.0, ALU.subtract, ALU.mult
                                   ).then_inc(rows_quantised, 1)

            pool.memset(minus_half[:], -0.5).then_inc(constants_set, 1)
            pool.memset(ones[:], 1.0).then_inc(constants_set, 1)
            pool.wait_ge(constants_set, 2)
            root(GROUPS, 1)
            root(GROUPS, 2)
            split_low(0, 0)
            group("first", 0)
            with pool.Fori(1, GROUPS - 1) as g:
                group("middle", g)
            group("last", GROUPS - 1)
            root(1, 2 + 2 * (GROUPS - 1) + 1)
            root(1, 2 + 2 * (GROUPS - 1) + 2)
            round_rows(GROUPS - 1)
            scales(GROUPS - 1)
            round_hidden(GROUPS - 1)

        @block.scalar
        def _(act):
            def high_part(g, u):
                s = SLOTS * g + u - 2
                v, b = (u - 2) % TILES, NB * g + (u - 2) // TILES
                act.wait_ge(probsT_ready, s + 1)
                wait(act, attn_ready, 2 * (b - 1) + (1 if v <= TA else 2))
                c = LATE_C if v == TA else CH
                nc.scalar.copy(pT_hi[0:CR, 0:c, v * P:(v + 1) * P], probsT[0:CR, 0:c, :]).then_inc(pT_hi_ready, 1)

            def late_high(g, u):
                b = NB * g + (u - 2) // TILES
                wait(act, attn_ready, 2 * (b - 1) + 2)
                nc.scalar.copy(pT_hi[0:CR, LATE_C:CH, TA * P:(TA + 1) * P], probsT[0:CR, LATE_C:CH, :]
                               ).then_inc(late_hi_ready, 1)

            def exps(g, u):
                s, par = SLOTS * g + u, u % 2
                act.wait_ge(neg_max_ready, s + 1)
                for k in range(BANKS):
                    n, at = (BANK + 1, last_bank_at(u % TILES)) if k == BANKS - 1 else (BANK, 0)
                    nc.scalar.activation(probs[:, par, k * BANK:k * BANK + n], scores[:, k, at:at + n], ACT.Exp,
                                         bias=neg_max[:, par:par + 1],
                                         accum_out=part_sum[:, par, k:k + 1]).then_inc(exp_done, 1)

            def round_qk(k, bank, rounded):
                e, h = k // 2, HEADS * (k % 2)
                src = bank[:, 0:HEADS * GR].rearrange("p (h j t i) -> p h j t i", h=HEADS, j=NB, i=QT)
                nc.scalar.copy(by_head(qk_next[:], e)[:, h:h + HEADS], src[:, :, 1]).then_inc(qk_stashed, 1)
                nc.scalar.copy(by_head(qk_hi[:, 0, :], e)[:, h:h + HEADS], src[:, :, 0]).then_inc(rounded, 1)

            def side_step(name, sides, g, par):
                n, r = sides.take(name)
                if name in ("o", "wsum", "nvoT", "nvo", "up", "down"):
                    return
                act.wait_ge(side_filled, n + 1)
                if name in ("ct0", "ct1", "ct2"):
                    k = int(name[2])
                    nc.scalar.copy(ctxT_hi[:, par, k * BANK:(k + 1) * BANK], side[:, 0:BANK]
                                   ).then_inc(side_rounded, 1)
                elif name[0:2] == "qk":
                    if name == "qk0":
                        act.wait_ge(qk_split, 2 * g + 2)
                    round_qk(int(name[2]), side, side_rounded)
                elif name in ("u0", "u1"):
                    k = int(name[1])
                    nc.scalar.copy(uT[:, 4 * k:4 * k + 4, :], side[:, 0:4 * GR].rearrange("p (h n) -> p h n", h=4)
                                   ).then_inc(side_drained, 1)
                elif name == "xt":
                    nc.scalar.copy(yqT[:, 0:GR], side16[:, 0:GR]).then_inc(side_drained, 1)
                elif name == "gate":
                    act.wait_ge(scales_ready, g)
                    nc.scalar.activation(hidden, side[0:GR, :], ACT.Tanh, scale=f[0:GR, 4:5]).then_inc(side_tanh, 1)
                elif name == "ht":
                    nc.scalar.copy(hqT[:, :, 0:GR], side16[:, 0:FF].rearrange("p (k n) -> p k n", n=P)[:, :, 0:GR]
                                   ).then_inc(side_drained, 1)
                elif name in ("wgT", "wuT", "wdT"):
                    dst = {"wgT": ff_gate, "wuT": ff_up, "wdT": ff_down}[name]
                    nc.scalar.copy(dst[:], side16[:, 0:FF]).then_inc(side_drained, 1)

            def drain_attn(kind, g, u):
                j, v = divmod(u, TILES)
                b = NB * g + j - 1
                second = v == 5
                act.wait_ge(attn_ready, 2 * b + 1 + second)
                base = ROWS * ((j + 1) % 2)
                lo, hi = part_columns(kind if u >= SLOTS else "", (j + 1) % 2, second)
                nc.scalar.copy(attnT[:, base + lo:base + hi], attn[:, 0:hi - lo]).then_inc(attn_drained, 1)

            def group(kind, g):
                sides = Sides(kind, g)
                for u in range(SLOTS):
                    j, v = divmod(u, TILES)
                    for name in steps_at(kind, u, 0):
                        side_step(name, sides, g, (j + 1) % 2)
                    if kind != "first" or u >= 2:
                        high_part(g, u)
                    for name in steps_at(kind, u, 1):
                        if name in EARLY:
                            side_step(name, sides, g, (j + 1) % 2)
                    exps(g, u)
                    for name in steps_at(kind, u, 1):
                        if name not in EARLY:
                            side_step(name, sides, g, (j + 1) % 2)
                    if v == TA + 2:
                        late_high(g, u)
                    if v in (1, 5) and (kind != "first" or j == 1):
                        drain_attn(kind, g, u)

            copied = [0]
            for n, (lane, name, bank) in enumerate(START):
                if lane == "read":
                    continue
                act.wait_ge(start_filled, n + 1)
                k = int(name[-1])
                if name[0:2] in ("wq", "wk"):
                    dst = wqT if name[1] == "q" else wkT
                    nc.scalar.copy(dst[:, 4 * k:4 * k + 4, :].rearrange("p h d -> p (h d)"), bank_of(bank)
                                   ).then_inc(start_copied, 1)
                elif name[0:2] == "wf":
                    if k == 0:
                        act.wait_ge(ctx_loaded, 16)
                        nc.scalar.copy(ctx_hi[0:CR, 0, :, :], raw[0:CR, :, :]).then_inc(ctx_split, 1)
                    nc.scalar.activation(fold[:, 4 * k:4 * k + 4, :].rearrange("p h d -> p (h d)"), bank_of(bank),
                                         ACT.Copy, scale=SCALE).then_inc(start_copied, 1)
                elif name[0:2] == "ct":
                    nc.scalar.copy(ctxT_hi[:, 0, k * BANK:(k + 1) * BANK], bank_of(bank)[:, 0:BANK]
                                   ).then_inc(start_rounded, 1)
                else:
                    round_qk(k, bank_of(bank), start_rounded)
            group("first", 0)
            with act.Fori(1, GROUPS - 1) as g:
                group("middle", g)
            group("last", GROUPS - 1)
            for u in (SLOTS, SLOTS + 1):
                high_part(GROUPS - 1, u)
            drain_attn("last", GROUPS - 1, SLOTS + 1)
            drain_attn("last", GROUPS - 1, SLOTS + 5)
            sides = Sides("end", GROUPS)
            for _, _, name in FINISH:
                side_step(name, sides, GROUPS, 0)

        @block.vector
        def _(dve):
            def max_banks(g, u):
                s, par = SLOTS * g + u, u % 2
                dve.wait_ge(scores_ready, 2 * s + 1)
                dve.tensor_reduce(part_max[:, par, 0:1], scores[:, 0:2, 0:BANK], AX.XY, ALU.max
                                  ).then_inc(maxima_found, 1)

            def max_last(g, u):
                s, par = SLOTS * g + u, u % 2
                dve.wait_ge(scores_ready, 2 * s + 2)
                at = last_bank_at(u % TILES)
                dve.tensor_reduce(part_max[:, par, 1:2], scores[:, 2, at:at + BANK + 1], AX.X, ALU.max
                                  ).then_inc(maxima_found, 1)
                dve.wait_ge(maxima_found, 2 * s + 2)
                dve.tensor_reduce(neg_max[:, par:par + 1], part_max[:, par, :], AX.X, ALU.max, negate=True
                                  ).then_inc(neg_max_ready, 1)

            def invert_sums(g, u):
                s, par = SLOTS * g + u, u % 2
                dve.wait_ge(exp_done, BANKS * (s + 1))
                dve.tensor_reduce(row_sum[:, par:par + 1], part_sum[:, par, :], AX.X, ALU.add).then_inc(sum_found, 1)
                dve.wait_ge(sum_found, s + 1)
                dve.reciprocal(inv_sum[:, par:par + 1], row_sum[:, par:par + 1]).then_inc(inv_ready, 1)

            def low_part(g, u):
                s, v = SLOTS * g + u - 2, (u - 2) % TILES
                dve.wait_ge(pT_hi_ready, s + 1)
                c = LATE_C if v == TA else CH
                cols = slice(v * P, (v + 1) * P)
                dve.tensor_tensor(pT_lo[0:CR, 0:c, cols], probsT[0:CR, 0:c, :], pT_hi[0:CR, 0:c, cols].bitcast(F32),
                                  ALU.subtract).then_inc(pT_lo_ready, 1)

            def late_low(g, u):
                dve.wait_ge(late_hi_ready, NB * g + (u - 2) // TILES + 1)
                cols = slice(TA * P, (TA + 1) * P)
                dve.tensor_tensor(pT_lo[0:CR, LATE_C:CH, cols], probsT[0:CR, LATE_C:CH, :],
                                  pT_hi[0:CR, LATE_C:CH, cols].bitcast(F32), ALU.subtract).then_inc(late_lo_ready, 1)

            def split_high(batch, par):
                dve.wait_ge(ctx_loaded, 16 * (batch + 1))
                wait(dve, attn_ready, 2 * (batch - 1))
                dve.tensor_copy(ctx_hi[0:CR, par, :, :], raw[0:CR, :, :]).then_inc(ctx_split, 1)

            fin = [0, 0]

            def step(ins):
                fin[1] += 1
                ins.then_inc(finish_step, 1)

            def chain(ins):
                step(ins)
                dve.wait_ge(finish_step, FINISH_OPS * fin[0] + fin[1])

            def moments(src):
                chain(dve.bn_stats(stats[0:GR, 0, :], src))
                dve.memset(f[0:GR, 15:16], 0.0)
                chain(dve.bn_aggr(f[0:GR, 0:2], stats[0:GR, 0, :]))
                dve.tensor_scalar(ve[0:GR, 0:1], f[0:GR, 1:2], EPS, None, ALU.add).then_inc(root_asked, 1)

            def stable_norm(n):
                o = side[0:GR, 0:D]
                chain(dve.tensor_reduce(f[0:GR, 2:3], o, AX.X, ALU.max))
                chain(dve.reciprocal(f[0:GR, 3:4], f[0:GR, 2:3]))
                dve.tensor_scalar(z[0:GR, :], o, f[0:GR, 3:4], None, ALU.mult).then_inc(side_drained, 1)

            def norm_moments(n):
                dve.wait_ge(side_drained, n + 1)
                moments(z[0:GR, :])

            def residual(grp):
                chain(dve.scalar_tensor_tensor(z[0:GR, :], z[0:GR, :], f[0:GR, 0:1], gout[0:GR, :],
                                               ALU.subtract, ALU.mult))
                dve.wait_ge(root_done, 2 + 2 * grp + 1)
                chain(dve.scalar_tensor_tensor(x2[0:GR, :], z[0:GR, :], rstd[0:GR, 0:1], row(xin, grp),
                                               ALU.mult, ALU.add))
                moments(x2[0:GR, :])

            def centre():
                chain(dve.tensor_scalar(z[0:GR, :], x2[0:GR, :], f[0:GR, 0:1], None, ALU.subtract))
                chain(dve.tensor_reduce(f[0:GR, 2:3], z[0:GR, :], AX.X, ALU.max, apply_absolute_value=True))

            def quantise_rows(grp):
                dve.wait_ge(root_done, 2 + 2 * grp + 2)
                chain(dve.tensor_scalar(f[0:GR, 6:7], f[0:GR, 2:3], rstd[0:GR, 0:1], EPS, ALU.mult, ALU.max))
                chain(dve.tensor_scalar(f[0:GR, 7:8], f[0:GR, 6:7], 1.0 / 127.0, None, ALU.mult))
                dve.reciprocal(f[0:GR, 3:4], f[0:GR, 7:8]).then_inc(rounding_asked, 1)

            def hidden_size():
                chain(dve.tensor_reduce(f[0:GR, 2:3], hidden, AX.X, ALU.max, apply_absolute_value=True))

            def quantise_hidden():
                chain(dve.tensor_scalar(f[0:GR, 7:8], f[0:GR, 2:3], EPS, 1.0 / 127.0, ALU.max, ALU.mult))
                dve.reciprocal(f[0:GR, 3:4], f[0:GR, 7:8]).then_inc(rounding_asked, 1)
                step(dve.tensor_scalar(f[0:GR, 8:9], wmean[0:GR, 2:3], f[0:GR, 7:8], None, ALU.mult))

            def finish_between(u, grp, o_step):
                if u == 8:
                    norm_moments(o_step)
                elif u == 9:
                    centre()
                elif u == 12:
                    quantise_hidden()

            def finish_after(u, grp):
                if u == 8:
                    residual(grp)
                elif u == 9:
                    quantise_rows(grp)
                elif u == 11:
                    hidden_size()

            def low_ctxT(k, par, bank, drained):
                cols = slice(k * BANK, (k + 1) * BANK)
                dve.tensor_tensor(ctxT_lo[:, par, cols], bank[:, 0:BANK], ctxT_hi[:, par, cols].bitcast(F32),
                                  ALU.subtract).then_inc(drained, 1)

            def low_qk(k, bank, drained):
                e, h = k // 2, HEADS * (k % 2)
                src = bank[:, 0:HEADS * GR].rearrange("p (h j t i) -> p h j t i", h=HEADS, j=NB, i=QT)
                dve.tensor_tensor(by_head(qk_lo[:, 0, :], e)[:, h:h + HEADS], src[:, :, 0],
                                  by_head(qk_hi[:, 0, :], e)[:, h:h + HEADS].bitcast(F32), ALU.subtract
                                  ).then_inc(drained, 1)

            def split_high_qk(g):
                dve.wait_ge(qk_stashed, 4 * (g + 1))
                dve.tensor_copy(qk_hi[:, 1, :], qk_next[:]).then_inc(qk_split, 1)

            def side_step(name, sides, g, par):
                n, r = sides.take(name)
                grp = g - 1
                if name in SPLIT:
                    dve.wait_ge(side_rounded, r + 1)
                    if name[0] == "c":
                        low_ctxT(int(name[2]), par, side, side_drained)
                    else:
                        dve.wait_ge(qk_stashed, 4 * (g + 1) + int(name[2]) + 1)
                        low_qk(int(name[2]), side, side_drained)
                elif name == "wsum":
                    dve.wait_ge(side_filled, n + 1)
                    dve.tensor_scalar(wmean[:], side[:, 0:3], 1.0 / (FF * D), EPS, ALU.mult, ALU.max
                                      ).then_inc(side_drained, 1)
                    dve.wait_ge(side_drained, n + 1)
                    dve.reciprocal(wscale[:], wmean[:]).then_inc(weights_step, 1)
                    quantise_weights(0, None)
                elif name in ("wgT", "wuT"):
                    dve.wait_ge(side_filled, n + 1)
                    quantise_weights(1 if name == "wgT" else 2, n)
                elif name in ("nvoT", "nvo"):
                    dve.wait_ge(side_filled, n + 1)
                    dve.tensor_copy(nvo[:], side[:, 0:D]).then_inc(side_drained, 1)
                elif name == "u0":
                    dve.wait_ge(probs_ready, 2 * SLOTS * g)
                    cols = null_probs[:, SLOTS * grp:SLOTS * g] if isinstance(grp, int) else \
                        null_probs[:, bass.ds(grp * SLOTS, SLOTS)]
                    dve.tensor_tensor(null_sel[:], cols.unsqueeze(2).broadcast_to((P, SLOTS, QT)),
                                      sel[:].unsqueeze(1).broadcast_to((P, SLOTS, QT)), ALU.mult
                                      ).then_inc(null_sel_ready, 1)
                elif name == "o":
                    fin[0], fin[1] = grp, 0
                    dve.wait_ge(side_filled, n + 1)
                    stable_norm(n)
                elif name == "gate":
                    dve.wait_ge(side_tanh, grp + 1)
                    dve.scalar_tensor_tensor(hidden, hidden, 1.0, side[0:GR, :], ALU.add, ALU.mult
                                             ).then_inc(side_drained, 1)
                elif name == "up":
                    dve.wait_ge(side_filled, n + 1)
                    dve.scalar_tensor_tensor(hidden, hidden, f[0:GR, 5:6], side[0:GR, :], ALU.mult, ALU.mult
                                             ).then_inc(side_drained, 1)
                    dve.wait_ge(side_drained, n + 1)
                elif name == "down":
                    dve.wait_ge(side_filled, n + 1)
                    wait(dve, out_written, 16 * grp)
                    dve.wait_ge(finish_step, FINISH_OPS * grp + fin[1])
                    dve.scalar_tensor_tensor(result[0:GR, :], side[0:GR, 0:D], f[0:GR, 8:9], x2[0:GR, :],
                                             ALU.mult, ALU.add).then_inc(side_drained, 1)

            wst = [1]

            def weights_chain(ins):
                wst[0] += 1
                ins.then_inc(weights_step, 1)

            def sum_weights():
                dve.wait_ge(late_loaded, LATE)
                for k in range(3):
                    dve.tensor_reduce(wabs[:, k:k + 1], raw_ffn[:, k * FF:(k + 1) * FF], AX.X, ALU.add,
                                      apply_absolute_value=True).then_inc(weights_quantised, 1)
                dve.tensor_scalar(window, window, null_v[:, 0:1], None, ALU.mult).then_inc(weights_quantised, 1)

            def quantise_weights(k, n):
                w = raw_ffn[:, k * FF:(k + 1) * FF]
                dve.wait_ge(weights_step, 1)
                weights_chain(dve.tensor_scalar(w, w, wscale[:, k:k + 1], ROUND, ALU.mult, ALU.add))
                dve.wait_ge(weights_step, wst[0])
                weights_chain(dve.tensor_scalar(w, w, ROUND, 1.0, ALU.subtract, ALU.min))
                dve.wait_ge(weights_step, wst[0])
                dve.tensor_scalar(ff_q[:], w, -1.0, None, ALU.max).then_inc(weights_quantised, 1)

            def group(kind, g):
                sides = Sides(kind, g)
                o_step = sides.base + (steps_of(kind).index("o") if kind != "first" else 0)
                for u in range(SLOTS):
                    j, v = divmod(u, TILES)
                    max_banks(g, u)
                    for name in steps_at(kind, u, 0):
                        side_step(name, sides, g, (j + 1) % 2)
                    if kind != "first":
                        finish_between(u, g - 1, o_step)
                    max_last(g, u)
                    if "up" in steps_at(kind, u, 1):
                        side_step("up", sides, g, (j + 1) % 2)
                    if kind != "first" or u >= 2:
                        low_part(g, u)
                    for name in steps_at(kind, u, 1):
                        if name in SPLIT:
                            side_step(name, sides, g, (j + 1) % 2)
                    invert_sums(g, u)
                    if v == TA + 2:
                        late_low(g, u)
                    if u == 1:
                        split_high_qk(g)
                    if v == TILES - 1 and not (kind == "last" and j == NB - 1):
                        split_high(NB * g + j + 1, (j + 1) % 2)
                    if kind == "first" and u == 3:
                        sum_weights()
                    for name in steps_at(kind, u, 1):
                        if name not in SPLIT and name != "up":
                            side_step(name, sides, g, (j + 1) % 2)
                    if kind != "first":
                        finish_after(u, g - 1)

            steps = [0]

            def start_chain(instructions):
                for ins in instructions:
                    steps[0] += 1
                    ins.then_inc(start_step, 1)
                dve.wait_ge(start_step, steps[0])

            def start_moments(src):
                start_chain([dve.bn_stats(stats[0:GR, k, :], src[0:GR, k, :]) for k in range(GROUPS)])
                start_chain([dve.bn_aggr(mv[0:GR, k, :], stats[0:GR, k, :]) for k in range(GROUPS)])
                dve.tensor_scalar(ve[0:GR, :], mv[0:GR, :, 1], EPS, None, ALU.add).then_inc(root_asked, 1)

            dve.wait_ge(x_loaded, 16)
            start_moments(xin)
            dve.wait_ge(root_done, 1)
            start_chain([dve.tensor_scalar(xw[:, k, :], xin[0:GR, k, :], mv[0:GR, k, 0:1], rstd[0:GR, k:k + 1],
                                           ALU.subtract, ALU.mult) for k in range(GROUPS)])
            start_chain([dve.tensor_reduce(mxs[0:GR, :], xw, AX.X, ALU.max)])
            start_chain([dve.reciprocal(ve[0:GR, :], mxs[0:GR, :])])
            start_chain([dve.tensor_scalar(xw[:, k, :], xw[:, k, :], ve[0:GR, k:k + 1], None, ALU.mult)
                         for k in range(GROUPS)])
            start_moments(xw)
            dve.wait_ge(ident_loaded, 16)
            dve.tensor_copy(ident16[:], ident[:]).then_inc(xn_ready, 1)
            dve.wait_ge(small_loaded, SMALL)
            dve.tensor_scalar(halves[:], halves[:], null_k[:, 0:1], None, ALU.mult).then_inc(xn_ready, 1)
            dve.wait_ge(root_done, 2)
            for k in range(GROUPS):
                dve.tensor_scalar(xw[:, k, :], xw[:, k, :], mv[0:GR, k, 0:1], rstd[0:GR, k:k + 1],
                                  ALU.subtract, ALU.mult).then_inc(xn_ready, 1)
            names = [name for _, name, _ in START]
            for n in map(names.index, VECTOR_ORDER):
                lane, name, bank = START[n]
                src = bank_of(bank)
                if lane == "read":
                    dve.wait_ge(start_filled, n + 1)
                if name == "wnk":
                    dve.tensor_scalar(wnk, src[:, 0:H], SCALE, None, ALU.mult).then_inc(start_read, 1)
                elif name == "xT":
                    dve.tensor_scalar(xnT[:], src[:, 0:GROUPS * GR], gin[:, 0:1], None, ALU.mult
                                      ).then_inc(start_read, 1)
                elif name == "n0":
                    dve.tensor_copy(n0, src[0:H, 0:GROUPS * GR]).then_inc(start_read, 1)
                elif name == "n1":
                    slots = GROUPS * SLOTS
                    dve.tensor_tensor(null_rows, src[:, 0:GROUPS * GR].rearrange("p (s i) -> p s i", i=QT),
                                      sel[:].unsqueeze(1).broadcast_to((P, slots, QT)), ALU.mult
                                      ).then_inc(start_read, 1)
                    dve.wait_ge(start_read, 4)
                    dve.tensor_reduce(null_scores[:], null_rows, AX.X, ALU.add).then_inc(start_read, 1)
                elif lane == "split":
                    k = int(name[-1])
                    dve.wait_ge(start_rounded, k + 1 if name[0] == "c" else 3 + k + 1)
                    if name[0] == "c":
                        low_ctxT(k, 0, src, start_split)
                    else:
                        dve.wait_ge(qk_stashed, k + 1)
                        low_qk(k, src, start_split)
            group("first", 0)
            with dve.Fori(1, GROUPS - 1) as g:
                group("middle", g)
            group("last", GROUPS - 1)
            for u in (SLOTS, SLOTS + 1):
                low_part(GROUPS - 1, u)
            sides = Sides("end", GROUPS)
            for _, _, name in FINISH:
                if name == "xt":
                    norm_moments(sides.base + sides.n - 1)
                    residual(GROUPS - 1)
                    centre()
                    quantise_rows(GROUPS - 1)
                if name == "ht":
                    hidden_size()
                    quantise_hidden()
                side_step(name, sides, GROUPS, 0)
            assert fin[1] == FINISH_OPS, fin[1]

        @block.tensor
        def _(pe):
            def three_passes(out_ap, high, low, m_high, m_low, start, stop):
                nc.tensor.matmul(out_ap, high, m_high, start=start, stop=False)
                nc.tensor.matmul(out_ap, high, m_low, start=False, stop=False)
                return nc.tensor.matmul(out_ap, low, m_high, start=False, stop=stop)

            def score_banks(g, u, banks, prepared_at):
                j, v = divmod(u, TILES)
                s, par = SLOTS * g + u, j % 2
                if v == 0:
                    wait(pe, side_drained, prepared_at - (j == 0 and 0 in banks))
                    if j == 1 and 0 in banks:
                        pe.wait_ge(qk_split, 2 * g + 2)
                cols = slice(v * P, (v + 1) * P)
                for k in banks:
                    wait(pe, exp_done, BANKS * (s - 1) + k + 1)
                    keys = slice(k * BANK, (k + 1) * BANK)
                    at = last_bank_at(v) if k == BANKS - 1 else 0
                    if k == BANKS - 1 and at == 0:
                        n = min(AHEAD, TILES - v)
                        nc.tensor.matmul(scores[:, k, BANK:BANK + 2 * n - 1:2], ident[:],
                                         null_scores[:, s:s + n] if isinstance(s, int) else
                                         null_scores[:, bass.ds(s, n)], start=True, stop=True)
                    last = three_passes(scores[:, k, at:at + BANK], qk_hi[:, par, cols], qk_lo[:, par, cols],
                                        ctxT_hi[:, par, keys], ctxT_lo[:, par, keys], True, True)
                last.then_inc(scores_ready, 1)

            def transpose_probs(g, u):
                s, par = SLOTS * g + u - 2, u % 2
                j, v = divmod(u, TILES)
                pe.wait_ge(probs_ready, 2 * (s + 1))
                wait(pe, pT_lo_ready, s)
                for c in range(CH):
                    if c == LATE_C and v == TA + 3:
                        pe.wait_ge(late_lo_ready, NB * g + j + 1)
                    last = nc.tensor.transpose(probsT[0:CR, c, :], probs[:, par, c * CR:(c + 1) * CR], ident[:])
                last.then_inc(probsT_ready, 1)

            def probs_by_ctx(kind, g, u):
                j, v = divmod(u, TILES)
                if v == TILES - 1:
                    b, jb, first, part, parts = NB * g + j, j, True, 0, 3
                elif v < 2:
                    b, jb, first, part, parts = NB * g + j - 1, j - 1, True, v + 1, 3
                else:
                    b, jb, first, part, parts = NB * g + j - 1, j - 1, False, v - 2, 4
                par = jb % 2
                lo, hi = part_columns(kind if u >= SLOTS - 1 else "", jb % 2, not first)
                tiles = hi // P
                if part == 0:
                    pe.wait_ge(pT_lo_ready, SLOTS * g + TILES * (j - (not first)) + tiles)
                    wait(pe, attn_drained, 2 * b + (not first))
                    pe.wait_ge(ctx_split, 2 * (b + 1))
                per = CH // parts
                for c in range(part * per, (part + 1) * per):
                    pairs = ((ctx_hi, pT_hi), (ctx_lo, pT_hi), (ctx_hi, pT_lo))
                    for i, (w, m) in enumerate(pairs):
                        last = nc.tensor.matmul(attn[:, 0:hi - lo], w[0:CR, par, c, :], m[0:CR, c, lo:hi],
                                                start=(c == 0 and i == 0), stop=(c == CH - 1 and i == 2))
                if part == parts - 1:
                    last.then_inc(attn_ready, 1)

            def transpose_ctx(k, bank):
                for i in range(CB):
                    last = nc.tensor.transpose(bank[:, i * CR:(i + 1) * CR], raw[0:CR, CB * k + i, :],
                                               ident[0:CR, 0:CR])
                return last

            def fold_queries(k, rows, bank):
                for i in range(HEADS):
                    last = nc.tensor.matmul(bank[:, i * GR:(i + 1) * GR], fold[:, HEADS * k + i, :], rows, start=True, stop=True)
                return last

            def side_step(name, sides, g, j):
                n, _ = sides.take(name)
                wait(pe, side_drained, n)
                if name in ("ct0", "ct1", "ct2"):
                    pe.wait_ge(ctx_loaded, 16 * (NB * g + j + 2))
                    last = transpose_ctx(int(name[2]), side)
                elif name[0:2] == "qk":
                    at = GR * (g + 1)
                    last = fold_queries(int(name[2]), xnT[:, at:at + GR] if isinstance(at, int) else
                                        xnT[:, bass.ds(at, GR)], side)
                elif name in ("u0", "u1"):
                    k = int(name[1])
                    if k == 0:
                        pe.wait_ge(attn_drained, 2 * NB * g)
                    for h in range(4 * k, 4 * k + 4):
                        for e in range(2):
                            last = nc.tensor.matmul(
                                side[e * DH:(e + 1) * DH, (h % 4) * GR:(h % 4 + 1) * GR],
                                wv[:, h * P + e * DH:h * P + (e + 1) * DH], attn_by_head[:, :, e, :, h],
                                start=True, stop=True)
                elif name == "o":
                    pe.wait_ge(null_sel_ready, g)
                    nc.tensor.matmul(side[0:GR, 0:D], null_sel[:].rearrange("p s i -> p (s i)"), nvo[:],
                                     start=True, stop=False)
                    for h in range(PAIRS):
                        last = nc.tensor.matmul(side[0:GR, 0:D], uT[:, h, :], wo[:, h, :],
                                                start=False, stop=(h == PAIRS - 1))
                elif name == "xt":
                    pe.wait_ge(rows_quantised, 2 * g - 1)
                    last = nc.tensor.transpose(side16[:, 0:GR], yq[0:GR, :], ident16[0:GR, 0:GR])
                elif name in ("gate", "up"):
                    w = ff_gate if name == "gate" else ff_up
                    last = nc.tensor.matmul(side[0:GR, :], yqT[:, 0:GR], w[:], start=True, stop=True)
                elif name == "ht":
                    pe.wait_ge(rows_quantised, 2 * g)
                    for k in range(FF // P):
                        last = nc.tensor.transpose(side16[:, k * P:k * P + GR], ff_q[0:GR, k * P:(k + 1) * P],
                                                   ident16[0:GR, 0:GR])
                elif name == "down":
                    for k in range(FF // P):
                        last = nc.tensor.matmul(side[0:GR, 0:D], hqT[:, k, 0:GR], ff_down[:, k * P:(k + 1) * P],
                                                start=(k == 0), stop=(k == FF // P - 1))
                elif name == "wsum":
                    pe.wait_ge(weights_quantised, 4)
                    last = nc.tensor.matmul(side[:, 0:3], ones[:], wabs[:], start=True, stop=True)
                elif name in ("wgT", "wuT", "wdT"):
                    pe.wait_ge(weights_quantised, 5 + ("wgT", "wuT", "wdT").index(name))
                    for k in range(FF // P):
                        last = nc.tensor.transpose(side16[:, k * P:(k + 1) * P], ff_q[:, k * P:(k + 1) * P],
                                                   ident16[:])
                elif name == "nvoT":
                    for h in range(PAIRS):
                        last = nc.tensor.matmul(side[:, 0:P], wo[:, h, :],
                                                window[:, :, PAIRS - 1 - h:2 * PAIRS - 1 - h],
                                                start=(h == 0), stop=(h == PAIRS - 1))
                elif name == "nvo":
                    last = nc.tensor.transpose(side[:, 0:D], nvo[:], ident[:])
                last.then_inc(side_filled, 1)

            def group(kind, g):
                sides = Sides(kind, g)
                prepared_at = sides.base
                for u in range(SLOTS):
                    j, v = divmod(u, TILES)
                    score_banks(g, u, (0, 1), prepared_at)
                    for name in steps_at(kind, u, 0):
                        side_step(name, sides, g, j)
                    if kind != "first" or u >= 2:
                        transpose_probs(g, u)
                    score_banks(g, u, (2,), prepared_at)
                    for name in steps_at(kind, u, 1):
                        side_step(name, sides, g, j)
                    if "ct2" in steps_at(kind, u, 0) + steps_at(kind, u, 1):
                        prepared_at = sides.base + sides.n
                    if kind != "first" or u >= TILES - 1:
                        probs_by_ctx(kind, g, u)

            pe.wait_ge(constants_set, 2)
            for _ in range(WARM):
                nc.tensor.matmul(attn[:, 0:P], ones[:], ones[:], start=True, stop=True)
            lanes = {"copy": 0, "read": 0, "split": 0}
            for n, (lane, name, bank) in enumerate(START):
                done, banks = {"copy": (start_copied, 3), "read": (start_read, 2), "split": (start_split, 3)}[lane]
                wait(pe, done, lanes[lane] - banks + 1)
                lanes[lane] += 1
                out_bank = bank_of(bank)
                k = int(name[-1]) if name[-1].isdigit() else 0
                if name[0:3] in ("wqT", "wkT"):
                    w, loaded = (wq, wq_loaded) if name[1] == "q" else (wk, wk_loaded)
                    pe.wait_ge(loaded, 16)
                    if n == 0:
                        pe.wait_ge(ident_loaded, 16)
                    for i in range(4):
                        c = (4 * k + i) * P
                        last = nc.tensor.transpose(out_bank[:, i * P:(i + 1) * P], w[:, c:c + P], ident[:])
                elif name[0:2] == "wf":
                    if k == 0:
                        pe.wait_ge(start_copied, 4)
                    for i in range(4):
                        e, hp = divmod(4 * k + i, PAIRS)
                        half = slice(e * DH, (e + 1) * DH)
                        last = nc.tensor.matmul(out_bank[:, i * P:(i + 1) * P], wqT[half, hp, :], wkT[half, hp, :],
                                                start=True, stop=True)
                elif name[0:2] == "ct":
                    pe.wait_ge(ctx_loaded, 16)
                    last = transpose_ctx(k, out_bank)
                elif name == "wnk":
                    pe.wait_ge(start_copied, 2)
                    for hp in range(PAIRS):
                        last = nc.tensor.matmul(out_bank[:, 2 * hp:2 * hp + 2], wqT[:, hp, :], halves[:],
                                                start=True, stop=True)
                elif name == "xT":
                    pe.wait_ge(xn_ready, 2 + GROUPS)
                    for i in range(GROUPS):
                        last = nc.tensor.transpose(out_bank[:, i * GR:(i + 1) * GR], xw[:, i, :],
                                                   ident[0:GR, 0:GR])
                elif name == "n0":
                    pe.wait_ge(start_read, 2)
                    last = nc.tensor.matmul(out_bank[0:H, 0:GROUPS * GR], wnk, xnT[:], start=True, stop=True)
                elif name == "n1":
                    pe.wait_ge(start_read, 3)
                    last = nc.tensor.matmul(out_bank[:, 0:GROUPS * GR], head_rows, n0, start=True, stop=True)
                else:
                    if k == 0:
                        pe.wait_ge(start_copied, 8)
                        pe.wait_ge(start_read, 1)
                    last = fold_queries(k, xnT[:, 0:GR], out_bank)
                last.then_inc(start_filled, 1)
            pe.wait_ge(start_split, 7)
            pe.wait_ge(start_read, 5)
            group("first", 0)
            with pe.Fori(1, GROUPS - 1) as g:
                group("middle", g)
            group("last", GROUPS - 1)
            for u in range(SLOTS, SLOTS + TILES - 1):
                if u < SLOTS + 2:
                    transpose_probs(GROUPS - 1, u)
                probs_by_ctx("last", GROUPS - 1, u)
            sides = Sides("end", GROUPS)
            for _, _, name in FINISH:
                side_step(name, sides, GROUPS, 0)


_INS = ["x", "ctx_1024", "L0_xattn_Wq", "L0_xattn_Wkv", "L0_xattn_Wo", "L0_xattn_g_in", "L0_xattn_g_out",
        "L0_xattn_null_kv", "L0_ffn_w_gate", "L0_ffn_w_up", "L0_ffn_w_down"]


def kernel(**inputs):
    import numpy as _np
    import concourse.bacc as _bacc
    from concourse import mybir as _mybir
    from concourse.bass_utils import run_bass_kernel_spmd as _run

    nc = _bacc.Bacc("TRN2", target_bir_lowering=False, num_devices=1)
    arrays = {n: _np.ascontiguousarray(inputs[n]) for n in _INS}
    r = _np.arange(P)
    arrays["identity"] = _np.eye(P, dtype=_np.float32)
    arrays["query_of"] = (((r % DH) // PAIRS)[:, None] == _np.arange(QT)[None, :]).astype(_np.float32)
    window = _np.zeros((P, 2, QT, 15), _np.float32)
    window[0:DH, 0, :, PAIRS - 1] = 1.0
    window[DH:P, 1, :, PAIRS - 1] = 1.0
    arrays["half_of"] = (r[:, None] // DH == _np.arange(2)[None, :]).astype(_np.float32)
    arrays["head_window"] = window.reshape(P, 16, 15)
    arrays["head_of"] = (_np.arange(H)[:, None] == (2 * (r % PAIRS) + r // DH)[None, :]).astype(_np.float32)
    args = [nc.dram_tensor(f"in_{n}_dram", a.shape, _mybir.dt.from_np(a.dtype), kind="ExternalInput").ap()
            for n, a in arrays.items()]
    out = nc.dram_tensor("out_0_dram", (B, N, D), _mybir.dt.float32, kind="ExternalOutput").ap()
    build(nc, *args, out)
    got = _run(nc, [{f"in_{n}_dram": a for n, a in arrays.items()}], core_ids=[0])
    return got.results[0]["out_0_dram"]
```

```python
from contextlib import ExitStack

import concourse.bass as bass
from concourse import mybir

ALU = mybir.AluOpType
ACT = mybir.ActivationFunctionType
AX = mybir.AxisListType
F32 = mybir.dt.float32
F32R = mybir.dt.float32r
BF16 = mybir.dt.bfloat16

P = 128
B, N, D = 8, 56, 128
M = 1500
H, DH = 16, 64
INNER = H * DH
FF = 512
PAIRS = H // 2
QT = P // H
TILES = N // QT
ROWS = TILES * P
CH, CR = 12, 125
BANK, BANKS = 500, 3
CB = CH // BANKS
NB = 2
GROUPS = B // NB
GR = NB * N
SLOTS = NB * TILES
AHEAD = 4
TA, TA_LAST = 3, 4
LATE_C = 8
EPS = 1e-5
ROUND = 1.5 * 2.0 ** 23
SCALE = DH ** -0.5


START = [("copy", "wqT0", ("probsT", 0)), ("copy", "wqT1", ("probsT", 1)),
         ("copy", "wkT0", ("probsT", 2)), ("copy", "wkT1", ("probsT", 0)),
         ("copy", "wf0", ("probsT", 1)), ("copy", "wf1", ("probsT", 2)),
         ("copy", "wf2", ("probsT", 0)), ("copy", "wf3", ("probsT", 1)),
         ("split", "ct0", ("scores", 0)), ("read", "xT", ("attn", 0)),
         ("split", "ct1", ("scores", 1)), ("split", "ct2", ("scores", 2)),
         ("split", "qk0", ("probsT", 0)), ("read", "n0", ("side", 0)),
         ("split", "qk1", ("probsT", 1)), ("split", "qk2", ("probsT", 2)), ("split", "qk3", ("probsT", 0)),
         ("read", "n1", ("attn", 0))]
VECTOR_ORDER = ("xT", "ct0", "ct1", "ct2", "qk0", "n0", "qk1", "qk2", "qk3", "n1")
WARM = 10
WARM_SLOT = 6
N_START = len(START)

PREP = [(2, 0, "ct0"), (3, 0, "ct1"), (4, 0, "ct2"), (10, 0, "ct0"), (12, 0, "ct1"), (12, 1, "ct2")]
FOLD = [(8, 0, "qk0"), (8, 1, "qk1"), (9, 0, "qk2"), (9, 1, "qk3")]
FINISH = [(6, 1, "u0"), (7, 0, "u1"), (7, 1, "o"), (10, 1, "xt"), (11, 0, "gate"), (11, 1, "up"),
          (13, 0, "ht"), (13, 1, "down")]
WEIGHTS = [(3, 1, "wsum"), (5, 1, "wgT"), (6, 1, "wuT"), (7, 1, "wdT"), (11, 0, "nvoT"), (13, 0, "nvo")]
PREP_FIRST = [(1, 0, "ct0"), (1, 1, "ct1"), (2, 0, "ct2")] + PREP[3:]
SPLIT = ("qk0", "qk1", "qk2", "qk3", "ct0", "ct1", "ct2")
EARLY = ("ct0", "ct1", "ct2", "qk0", "qk1", "qk2", "qk3", "xt")
APART = ("u1", "o", "up")
HEADS = 4
POOL_OPS = 4
FINISH_OPS = 15


def steps_at(kind, u, place):
    steps = WEIGHTS if kind == "first" else FINISH
    if kind == "last":
        steps = steps + [x for x in PREP if x[0] < TILES]
    else:
        steps = steps + FOLD + (PREP_FIRST if kind == "first" else PREP)
    return [n for s, p, n in steps if (s, p) == (u, place)]


def steps_of(kind):
    return [n for u in range(SLOTS) for place in (0, 1) for n in steps_at(kind, u, place)]


N_FIRST, N_MIDDLE = len(steps_of("first")), len(steps_of("middle"))
N_SPLIT = len(PREP) + len(FOLD)


class Sides:

    def __init__(self, kind, g):
        self.n = self.split = 0
        self.base = 0 if kind == "first" else N_FIRST + N_MIDDLE * (g - 1)
        self.split_base = N_SPLIT * g
        if kind == "end":
            self.base = N_FIRST + N_MIDDLE * (GROUPS - 2) + len(steps_of("last"))

    def take(self, name):
        self.n += 1
        self.split += name in SPLIT
        return self.base + (self.n - 1), self.split_base + (self.split - 1)


def part_columns(kind, j, second):
    at = P * (TA_LAST if kind == "last" and j == NB - 1 else TA)
    return (at, ROWS) if second else (0, at)


def last_bank_at(v):
    return 2 * (v % AHEAD)


def wait(eng, semaphore, value):
    if isinstance(value, int) and value <= 0:
        return
    eng.wait_ge(semaphore, value)


def row(tensor, index):
    if isinstance(index, int):
        return tensor[0:GR, index, :]
    return tensor[0:GR, bass.ds(index, 1), :].rearrange("p a d -> p (a d)")


def build(nc, x, ctx, Wq, Wkv, Wo, g_in, g_out, null_kv, w_gate, w_up, w_down,
          identity, query_of, head_window, head_of, out):
    with ExitStack() as stack:
        def sb(name, shape, dt=F32):
            return stack.enter_context(nc.sbuf_tensor(name, shape, dt))

        def psum(name, shape, dt=F32):
            return stack.enter_context(nc.psum_tensor(name, shape, dt))

        def sem(name):
            return stack.enter_context(nc.semaphore(name))

        scores = psum("scores", [P, BANKS, 512])
        probsT = psum("probsT", [P, CH, P])
        attn = psum("attn", [P, 512])
        side = psum("side", [P, 512])
        side16 = side[:].bitcast(BF16)

        def side_bank(kind, name):
            if kind != "end" or name not in APART:
                return side[:]
            return attn[:] if name == "o" else probsT[:, 0:4, :].rearrange("p c n -> p (c n)")

        raw = sb("raw", [P, CH, D])
        ctx_hi = sb("ctx_hi", [P, 2, CH, D], F32R)
        ctx_lo = sb("ctx_lo", [P, 2, CH, D], F32R)
        ctxT_hi = sb("ctxT_hi", [P, 2, M], F32R)
        ctxT_lo = sb("ctxT_lo", [P, 2, M], F32R)
        qk_hi = sb("qk_hi", [P, 2, ROWS], F32R)
        qk_lo = sb("qk_lo", [P, 2, ROWS], F32R)
        qk_next = sb("qk_next", [P, ROWS])
        probs = sb("probs", [P, 2, M + 4])
        pT_hi = sb("pT_hi", [P, CH, ROWS], F32R)
        pT_lo = sb("pT_lo", [P, CH, ROWS], F32R)
        attnT = sb("attnT", [P, NB * ROWS])
        null_probs = sb("null_probs", [P, GROUPS * SLOTS])
        null_sel = sb("null_sel", [P, SLOTS, QT])
        fold = sb("fold", [P, H, D])
        wv = sb("wv", [P, INNER])
        wo = sb("wo", [P, PAIRS, D])
        ff_gate = sb("ff_gate", [P, FF], BF16)
        ff_up = sb("ff_up", [P, FF], BF16)
        ff_down = sb("ff_down", [P, FF], BF16)
        ff_q = sb("ff_q", [P, FF], BF16)
        work = sb("work", [P, 9 * D])
        uT = work[:, 0:PAIRS * GR].rearrange("p (h n) -> p h n", h=PAIRS)
        x2 = work[:, 0:D]
        hqT = work[:, D:3 * D].bitcast(BF16).rearrange("p (k n) -> p k n", n=P)
        yq = work[:, 3 * D:3 * D + D // 2].bitcast(BF16)
        yqT = work[:, 3 * D + D // 2:4 * D].bitcast(BF16)
        hidden = work[0:GR, 4 * D:8 * D]
        z = work[:, 8 * D:9 * D]
        ident = sb("ident", [P, P])
        ident16 = sb("ident16", [P, P], BF16)
        ones = sb("ones", [P, P])
        sel = sb("sel", [P, QT])
        null_v = sb("null_v", [P, 1])
        null_k = sb("null_k", [P, DH])
        null_scores = sb("null_scores", [P, GROUPS * SLOTS])
        nvo = sb("nvo", [P, D])
        gin = sb("gin", [P, 1])
        gout = sb("gout", [P, D])
        result = sb("result", [P, D])
        xin = sb("xin", [P, GROUPS, D])
        xnT = sb("xnT", [P, GROUPS * GR])
        wq = probs[:, 0, 0:INNER]
        wk = probs[:, 1, 0:INNER]
        wqT = attnT[:, 0:INNER].rearrange("p (h d) -> p h d", h=PAIRS)
        wkT = work[:, 0:INNER].rearrange("p (h d) -> p h d", h=PAIRS)
        xw = attnT[0:GR, INNER:INNER + GROUPS * D].rearrange("p (g d) -> p g d", g=GROUPS)
        window = attnT[:, INNER + GROUPS * D:INNER + GROUPS * D + 240].rearrange("p (a b) -> p a b", b=15)
        raw_ffn = attnT[:, 0:3 * FF]
        wnk = result[:, 0:H]
        wq_null = wv[:].rearrange("p (h d) -> p h d", h=H)
        head_rows = gout[0:H, :]
        n0 = probs[0:H, 0, INNER:INNER + GROUPS * GR]
        null_rows = probs[:, 1, INNER:INNER + GROUPS * GR].rearrange("p (s i) -> p s i", i=QT)
        stats = sb("stats", [P, GROUPS, 6])
        mv = sb("mv", [P, GROUPS, 2])
        ve = sb("ve", [P, GROUPS])
        rstd = sb("rstd", [P, GROUPS])
        row_max = sb("row_max", [P, GROUPS])
        minus_half = sb("minus_half", [P, GROUPS])
        part_max = sb("part_max", [P, 2, 2])
        neg_max = sb("neg_max", [P, 2])
        part_sum = sb("part_sum", [P, 2, BANKS])
        row_sum = sb("row_sum", [P, 2])
        inv_sum = sb("inv_sum", [P, 2])
        wabs = sb("wabs", [P, 3])
        wmean = sb("wmean", [P, 3])
        wscale = sb("wscale", [P, 3])
        f = sb("f", [P, 16])

        x_loaded = sem("x_loaded")
        ident_loaded = sem("ident_loaded")
        small_loaded = sem("small_loaded")
        null_loaded = sem("null_loaded")
        null_weighted = sem("null_weighted")
        wnk_ready = sem("wnk_ready")
        wk_loaded = sem("wk_loaded")
        wq_loaded = sem("wq_loaded")
        late_loaded = sem("late_loaded")
        ctx_loaded = sem("ctx_loaded")
        constants_set = sem("constants_set")
        start_step = sem("start_step")
        xn_ready = sem("xn_ready")
        start_filled = sem("start_filled")
        start_copied = sem("start_copied")
        start_read = sem("start_read")
        start_rounded = sem("start_rounded")
        start_split = sem("start_split")
        root_asked = sem("root_asked")
        root_done = sem("root_done")
        side_filled = sem("side_filled")
        side_drained = sem("side_drained")
        side_rounded = sem("side_rounded")
        side_tanh = sem("side_tanh")
        qk_stashed = sem("qk_stashed")
        qk_split = sem("qk_split")
        ctx_split = sem("ctx_split")
        scores_ready = sem("scores_ready")
        maxima_found = sem("maxima_found")
        neg_max_ready = sem("neg_max_ready")
        exp_done = sem("exp_done")
        sum_found = sem("sum_found")
        inv_ready = sem("inv_ready")
        probs_ready = sem("probs_ready")
        end_transposed = sem("end_transposed")
        end_hi_ready = sem("end_hi_ready")
        end_lo_ready = sem("end_lo_ready")
        late_hi_ready = sem("late_hi_ready")
        late_lo_ready = sem("late_lo_ready")
        probsT_ready = sem("probsT_ready")
        pT_hi_ready = sem("pT_hi_ready")
        pT_lo_ready = sem("pT_lo_ready")
        attn_ready = sem("attn_ready")
        attn_drained = sem("attn_drained")
        finish_step = sem("finish_step")
        window_set = sem("window_set")
        weights_summed = sem("weights_summed")
        scales_found = sem("scales_found")
        weights_step = sem("weights_step")
        weights_rounded = sem("weights_rounded")
        weights_quantised = sem("weights_quantised")
        rounding_asked = sem("rounding_asked")
        pool_step = sem("pool_step")
        scales_ready = sem("scales_ready")
        null_sel_ready = sem("null_sel_ready")
        rows_quantised = sem("rows_quantised")
        out_written = sem("out_written")

        x_rows = x.rearrange("b n d -> (b n) d")
        out_rows = out.rearrange("b n d -> (b n) d")
        ctx_v = ctx.rearrange("b (p c) d -> b p c d", c=CH)
        attn_by_head = attnT[:].rearrange("p (t e i h) -> p t e i h", e=2, i=QT, h=PAIRS)

        def by_head(a, e):
            return a.rearrange("p (t e i h) -> p e h t i", e=2, i=QT, h=PAIRS)[:, e]

        def bank_of(name):
            kind, k = name
            if kind == "probsT":
                return probsT[:].rearrange("p (k c) n -> p k (c n)", k=BANKS)[:, k]
            return {"scores": scores[:, k, :], "attn": attn[:], "side": side[:]}[kind]

        block = stack.enter_context(nc.Block())

        @block.sync
        def _(sp):
            sp.dma_start(xin[0:GR, :, :], x_rows.rearrange("(g p) d -> p g d", p=GR)).then_inc(x_loaded, 16)
            sp.dma_start(ident[:], identity).then_inc(ident_loaded, 16)
            sp.dma_start(wq, Wq).then_inc(wq_loaded, 16)
            sp.dma_start(null_k[:], null_kv[0:1, :].broadcast_to((P, DH))).then_inc(null_loaded, 16)
            sp.dma_start(wk, Wkv[:, 0:INNER]).then_inc(wk_loaded, 16)
            sp.dma_start(raw[0:CR, :, :], ctx_v[0]).then_inc(ctx_loaded, 16)
            sp.dma_start(gin[:], g_in.rearrange("(d a) -> d a", a=1)).then_inc(small_loaded, 16)
            sp.dma_start(head_rows, head_of).then_inc(small_loaded, 16)
            sp.dma_start(sel[:], query_of).then_inc(small_loaded, 16)

            def load(batch, transposed, count):
                sp.wait_ge(ctx_split, 2 * batch)
                sp.wait_ge(transposed, count)
                src = ctx_v[batch] if isinstance(batch, int) else \
                    ctx_v[bass.ds(batch, 1)].rearrange("a p c d -> p (a c) d")
                sp.dma_start(raw[0:CR, :, :], src).then_inc(ctx_loaded, 16)

            def store(group, kind):
                down = Sides(kind, group + 1).base + \
                    (steps_of(kind).index("down") if kind != "end" else len(FINISH) - 1)
                sp.wait_ge(side_drained, down + 1)
                dst = out_rows[GR * group:GR * group + GR, :] if isinstance(group, int) else \
                    out_rows[bass.ds(group * GR, GR), :]
                sp.dma_start(dst, result[0:GR, :]).then_inc(out_written, 16)

            load(1, start_rounded, 3)
            sp.wait_ge(start_filled, N_START)
            sp.wait_ge(start_read, 4)
            sp.dma_start(raw_ffn[:, 0:FF].rearrange("p (b d) -> p b d", d=D),
                         w_gate.rearrange("(b p) d -> p b d", p=P)).then_inc(late_loaded, 16)
            sp.dma_start(raw_ffn[:, FF:2 * FF].rearrange("p (b d) -> p b d", d=D),
                         w_up.rearrange("(b p) d -> p b d", p=P)).then_inc(late_loaded, 16)
            sp.dma_start(raw_ffn[:, 2 * FF:3 * FF], w_down).then_inc(late_loaded, 16)
            for e in range(2):
                sp.dma_start(null_v[e * DH:(e + 1) * DH, :], null_kv[1:2, :].rearrange("a d -> d a")
                             ).then_inc(late_loaded, 16)
            sp.dma_start(window, head_window).then_inc(late_loaded, 16)
            sp.dma_start(gout[0:GR, :], g_out.rearrange("(a d) -> a d", a=1).broadcast_to((GR, D))
                         ).then_inc(late_loaded, 16)
            sp.dma_start(wv[:], Wkv[:, INNER:2 * INNER]).then_inc(late_loaded, 16)
            sp.dma_start(wo[:], Wo.rearrange("(h p) d -> p h d", p=P)).then_inc(late_loaded, 16)
            load(2, side_rounded, 3)
            load(3, side_rounded, N_SPLIT)
            with sp.Fori(1, GROUPS - 1) as g:
                load(NB * g + 2, side_rounded, N_SPLIT * g + 3)
                store(g - 1, "middle")
                sp.wait_ge(out_written, 16 * g)
                load(NB * g + 3, side_rounded, N_SPLIT * (g + 1))
            store(GROUPS - 2, "last")
            store(GROUPS - 1, "end")
            sp.wait_ge(out_written, 16 * GROUPS)

        LATE = 16 * 9
        SMALL = 16 * 3

        @block.gpsimd
        def _(pool):
            def root(cols, count):
                pool.wait_ge(root_asked, count)
                pool.tensor_tensor(rstd[0:GR, 0:cols], ve[0:GR, 0:cols], minus_half[0:GR, 0:cols],
                                   ALU.pow).then_inc(root_done, 1)

            def split_low(batch, par):
                pool.wait_ge(ctx_split, 2 * batch + 1)
                pool.tensor_tensor(ctx_lo[0:CR, par, :, :], raw[0:CR, :, :], ctx_hi[0:CR, par, :, :].bitcast(F32),
                                   ALU.subtract).then_inc(ctx_split, 1)

            def split_low_qk(g):
                pool.wait_ge(qk_split, 2 * g + 1)
                pool.tensor_tensor(qk_lo[:, 1, :], qk_next[:], qk_hi[:, 1, :].bitcast(F32), ALU.subtract
                                   ).then_inc(qk_split, 1)

            def normalise(g, u):
                s, par = SLOTS * g + u, u % 2
                pool.wait_ge(inv_ready, s + 1)
                inv = inv_sum[:, par:par + 1]
                null_out = null_probs[:, s:s + 1] if isinstance(s, int) else null_probs[:, bass.ds(s, 1)]
                pool.tensor_tensor(null_out, probs[:, par, M:M + 1], inv, ALU.mult).then_inc(probs_ready, 1)
                pool.tensor_scalar(probs[:, par, 0:M], probs[:, par, 0:M], inv, 1.0, ALU.mult, ALU.mult
                                   ).then_inc(probs_ready, 1)

            def group(kind, g):
                for u in range(SLOTS):
                    j, v = divmod(u, TILES)
                    if kind != "first" and u in (8, 9):
                        root(1, 2 + 2 * (g - 1) + (u - 8) + 1)
                    if kind != "first" and u == 9:
                        round_rows(g - 1)
                    if kind != "first" and u == 12:
                        round_hidden(g - 1)
                    normalise(g, u)
                    if kind != "first" and u == 9:
                        scales(g - 1)
                    if u == 1:
                        split_low_qk(g)
                    if kind == "first" and u == 2:
                        null_window()
                    if kind == "first" and u in (3, 4, 5):
                        round_weights(u - 3)
                    if v == TILES - 1 and not (kind == "last" and j == NB - 1):
                        split_low(NB * g + j + 1, (j + 1) % 2)

            def carry():
                pool.tensor_tensor(f[0:GR, 14:15], minus_half[0:GR, 0:1], minus_half[0:GR, 0:1], ALU.mult)

            def null_window():
                pool.wait_ge(late_loaded, LATE)
                pool.tensor_scalar(window, window, null_v[:, 0:1], 1.0, ALU.mult, ALU.mult
                                   ).then_inc(window_set, 1)

            def round_weights(k):
                w = raw_ffn[:, k * FF:(k + 1) * FF]
                pool.wait_ge(scales_found, 1)
                pool.tensor_scalar(w, w, wscale[:, k:k + 1], ROUND, ALU.mult, ALU.add).then_inc(weights_step, 1)
                pool.wait_ge(weights_step, k + 1)
                pool.tensor_scalar(w, w, -ROUND, 1.0, ALU.add, ALU.mult).then_inc(weights_rounded, 1)

            def round_rows(grp):
                pool.wait_ge(rounding_asked, 2 * grp + 1)
                carry()
                pool.tensor_scalar(z[0:GR, :], z[0:GR, :], rstd[0:GR, 0:1], f[0:GR, 3:4], ALU.mult, ALU.mult
                                   ).then_inc(pool_step, 1)
                pool.wait_ge(pool_step, POOL_OPS * grp + 1)
                carry()
                pool.tensor_scalar(z[0:GR, :], z[0:GR, :], ROUND, 1.0, ALU.add, ALU.mult).then_inc(pool_step, 1)
                pool.wait_ge(pool_step, POOL_OPS * grp + 2)
                carry()
                pool.tensor_scalar(yq[0:GR, :], z[0:GR, :], -ROUND, 1.0, ALU.add, ALU.mult
                                   ).then_inc(rows_quantised, 1)

            def scales(grp):
                pool.tensor_scalar(f[0:GR, 4:5], wmean[0:GR, 0:1], f[0:GR, 7:8], 0.5, ALU.mult, ALU.mult
                                   ).then_inc(pool_step, 1)
                pool.wait_ge(pool_step, POOL_OPS * grp + 3)
                carry()
                pool.tensor_scalar(f[0:GR, 5:6], wmean[0:GR, 1:2], f[0:GR, 7:8], f[0:GR, 4:5],
                                   ALU.mult, ALU.mult).then_inc(scales_ready, 1)

            def round_hidden(grp):
                pool.wait_ge(rounding_asked, 2 * grp + 2)
                carry()
                pool.tensor_scalar(hidden, hidden, f[0:GR, 3:4], ROUND, ALU.mult, ALU.add).then_inc(pool_step, 1)
                pool.wait_ge(pool_step, POOL_OPS * grp + 4)
                carry()
                pool.tensor_scalar(ff_q[0:GR, :], hidden, -ROUND, 1.0, ALU.add, ALU.mult
                                   ).then_inc(rows_quantised, 1)

            pool.memset(minus_half[:], -0.5).then_inc(constants_set, 1)
            pool.memset(ones[:], 1.0).then_inc(constants_set, 1)
            pool.wait_ge(constants_set, 2)
            root(GROUPS, 1)
            pool.wait_ge(wq_loaded, 16)
            pool.wait_ge(null_loaded, 16)
            pool.tensor_tensor(wq_null, wq.rearrange("p (h d) -> p h d", h=H),
                               null_k[:].unsqueeze(1).broadcast_to((P, H, DH)), ALU.mult).then_inc(null_weighted, 1)
            root(GROUPS, 2)
            split_low(0, 0)
            group("first", 0)
            with pool.Fori(1, GROUPS - 1) as g:
                group("middle", g)
            group("last", GROUPS - 1)
            root(1, 2 + 2 * (GROUPS - 1) + 1)
            root(1, 2 + 2 * (GROUPS - 1) + 2)

        @block.scalar
        def _(act):
            def high_part(g, u):
                s = SLOTS * g + u - 2
                v, b = (u - 2) % TILES, NB * g + (u - 2) // TILES
                act.wait_ge(probsT_ready, s + 1)
                wait(act, attn_ready, 2 * (b - 1) + (1 if v <= TA else 2))
                c = LATE_C if v == TA else CH
                nc.scalar.copy(pT_hi[0:CR, 0:c, v * P:(v + 1) * P], probsT[0:CR, 0:c, :]).then_inc(pT_hi_ready, 1)

            def end_high(i):
                cols = slice((TILES - 2 + i) * P, (TILES - 1 + i) * P)
                for k in range(BANKS):
                    act.wait_ge(end_transposed, BANKS * i + k + 1)
                    c = slice(k * CB, (k + 1) * CB)
                    nc.scalar.copy(pT_hi[0:CR, c, cols], probsT[0:CR, c, :]).then_inc(end_hi_ready, 1)

            def late_high(g, u):
                b = NB * g + (u - 2) // TILES
                wait(act, attn_ready, 2 * (b - 1) + 2)
                nc.scalar.copy(pT_hi[0:CR, LATE_C:CH, TA * P:(TA + 1) * P], probsT[0:CR, LATE_C:CH, :]
                               ).then_inc(late_hi_ready, 1)

            def exps(g, u):
                s, par = SLOTS * g + u, u % 2
                act.wait_ge(neg_max_ready, s + 1)
                for k in range(BANKS):
                    n, at = (BANK + 1, last_bank_at(u % TILES)) if k == BANKS - 1 else (BANK, 0)
                    nc.scalar.activation(probs[:, par, k * BANK:k * BANK + n], scores[:, k, at:at + n], ACT.Exp,
                                         bias=neg_max[:, par:par + 1],
                                         accum_out=part_sum[:, par, k:k + 1]).then_inc(exp_done, 1)

            def round_qk(k, bank, rounded):
                e, h = k // 2, HEADS * (k % 2)
                src = bank[:, 0:HEADS * GR].rearrange("p (h j t i) -> p h j t i", h=HEADS, j=NB, i=QT)
                nc.scalar.copy(by_head(qk_next[:], e)[:, h:h + HEADS], src[:, :, 1]).then_inc(qk_stashed, 1)
                nc.scalar.copy(by_head(qk_hi[:, 0, :], e)[:, h:h + HEADS], src[:, :, 0]).then_inc(rounded, 1)

            def side_step(name, sides, g, par, kind=""):
                n, r = sides.take(name)
                bank = side_bank(kind, name)
                if name in ("o", "wsum", "nvoT", "nvo", "up", "down"):
                    return
                act.wait_ge(side_filled, n + 1)
                if name in ("ct0", "ct1", "ct2"):
                    k = int(name[2])
                    nc.scalar.copy(ctxT_hi[:, par, k * BANK:(k + 1) * BANK], side[:, 0:BANK]
                                   ).then_inc(side_rounded, 1)
                elif name[0:2] == "qk":
                    if name == "qk0":
                        act.wait_ge(qk_split, 2 * g + 2)
                    round_qk(int(name[2]), side, side_rounded)
                elif name in ("u0", "u1"):
                    k = int(name[1])
                    nc.scalar.copy(uT[:, 4 * k:4 * k + 4, :], bank[:, 0:4 * GR].rearrange("p (h n) -> p h n", h=4)
                                   ).then_inc(side_drained, 1)
                elif name == "xt":
                    nc.scalar.copy(yqT[:, 0:GR], side16[:, 0:GR]).then_inc(side_drained, 1)
                elif name == "gate":
                    act.wait_ge(scales_ready, g)
                    nc.scalar.activation(hidden, side[0:GR, :], ACT.Tanh, scale=f[0:GR, 4:5]).then_inc(side_tanh, 1)
                elif name == "ht":
                    nc.scalar.copy(hqT[:, :, 0:GR], side16[:, 0:FF].rearrange("p (k n) -> p k n", n=P)[:, :, 0:GR]
                                   ).then_inc(side_drained, 1)
                elif name in ("wgT", "wuT", "wdT"):
                    dst = {"wgT": ff_gate, "wuT": ff_up, "wdT": ff_down}[name]
                    nc.scalar.copy(dst[:], side16[:, 0:FF]).then_inc(side_drained, 1)

            def sum_weights():
                act.wait_ge(late_loaded, LATE)
                for k, unused in enumerate((work[:, 0:FF], work[:, FF:2 * FF], ff_down[:])):
                    nc.scalar.activation(unused, raw_ffn[:, k * FF:(k + 1) * FF], ACT.Abs,
                                         accum_out=wabs[:, k:k + 1]).then_inc(weights_summed, 1)

            def drain_attn(kind, g, u):
                j, v = divmod(u, TILES)
                b = NB * g + j - 1
                second = v == 5
                act.wait_ge(attn_ready, 2 * b + 1 + second)
                base = ROWS * ((j + 1) % 2)
                lo, hi = part_columns(kind if u >= SLOTS else "", (j + 1) % 2, second)
                bank = scores[:, 0, :] if u == SLOTS + 5 else attn[:]
                nc.scalar.copy(attnT[:, base + lo:base + hi], bank[:, 0:hi - lo]).then_inc(attn_drained, 1)

            def group(kind, g):
                sides = Sides(kind, g)
                for u in range(SLOTS):
                    j, v = divmod(u, TILES)
                    for name in steps_at(kind, u, 0):
                        side_step(name, sides, g, (j + 1) % 2)
                    if kind != "first" or u >= 2:
                        high_part(g, u)
                    for name in steps_at(kind, u, 1):
                        if name in EARLY:
                            side_step(name, sides, g, (j + 1) % 2)
                    exps(g, u)
                    for name in steps_at(kind, u, 1):
                        if name not in EARLY:
                            side_step(name, sides, g, (j + 1) % 2)
                    if kind == "first" and u == 2:
                        sum_weights()
                    if v == TA + 2:
                        late_high(g, u)
                    if v in (1, 5) and (kind != "first" or j == 1):
                        drain_attn(kind, g, u)

            for n, (lane, name, bank) in enumerate(START):
                if lane == "read":
                    continue
                if name == "wf0":
                    act.wait_ge(ctx_loaded, 16)
                    nc.scalar.copy(ctx_hi[0:CR, 0, :, :], raw[0:CR, :, :]).then_inc(ctx_split, 1)
                act.wait_ge(start_filled, n + 1)
                k = int(name[-1])
                if name[0:2] in ("wq", "wk"):
                    dst = wqT if name[1] == "q" else wkT
                    nc.scalar.copy(dst[:, 4 * k:4 * k + 4, :].rearrange("p h d -> p (h d)"), bank_of(bank)
                                   ).then_inc(start_copied, 1)
                elif name[0:2] == "wf":
                    nc.scalar.activation(fold[:, 4 * k:4 * k + 4, :].rearrange("p h d -> p (h d)"), bank_of(bank),
                                         ACT.Copy, scale=SCALE).then_inc(start_copied, 1)
                elif name[0:2] == "ct":
                    nc.scalar.copy(ctxT_hi[:, 0, k * BANK:(k + 1) * BANK], bank_of(bank)[:, 0:BANK]
                                   ).then_inc(start_rounded, 1)
                else:
                    round_qk(k, bank_of(bank), start_rounded)
            group("first", 0)
            with act.Fori(1, GROUPS - 1) as g:
                group("middle", g)
            group("last", GROUPS - 1)
            act.wait_ge(attn_ready, 2 * (B - 1))
            for i in range(2):
                end_high(i)
            drain_attn("last", GROUPS - 1, SLOTS + 1)
            drain_attn("last", GROUPS - 1, SLOTS + 5)
            sides = Sides("end", GROUPS)
            for _, _, name in FINISH:
                side_step(name, sides, GROUPS, 0, "end")

        @block.vector
        def _(dve):
            def max_banks(g, u):
                s, par = SLOTS * g + u, u % 2
                dve.wait_ge(scores_ready, 2 * s + 1)
                dve.tensor_reduce(part_max[:, par, 0:1], scores[:, 0:2, 0:BANK], AX.XY, ALU.max
                                  ).then_inc(maxima_found, 1)

            def max_last(g, u):
                s, par = SLOTS * g + u, u % 2
                dve.wait_ge(scores_ready, 2 * s + 2)
                at = last_bank_at(u % TILES)
                dve.tensor_reduce(part_max[:, par, 1:2], scores[:, 2, at:at + BANK + 1], AX.X, ALU.max
                                  ).then_inc(maxima_found, 1)
                dve.wait_ge(maxima_found, 2 * s + 2)
                dve.tensor_reduce(neg_max[:, par:par + 1], part_max[:, par, :], AX.X, ALU.max, negate=True
                                  ).then_inc(neg_max_ready, 1)

            def invert_sums(g, u):
                s, par = SLOTS * g + u, u % 2
                dve.wait_ge(exp_done, BANKS * (s + 1))
                dve.tensor_reduce(row_sum[:, par:par + 1], part_sum[:, par, :], AX.X, ALU.add).then_inc(sum_found, 1)
                dve.wait_ge(sum_found, s + 1)
                dve.reciprocal(inv_sum[:, par:par + 1], row_sum[:, par:par + 1]).then_inc(inv_ready, 1)

            def low_part(g, u):
                s, v = SLOTS * g + u - 2, (u - 2) % TILES
                dve.wait_ge(pT_hi_ready, s + 1)
                c = LATE_C if v == TA else CH
                cols = slice(v * P, (v + 1) * P)
                dve.tensor_tensor(pT_lo[0:CR, 0:c, cols], probsT[0:CR, 0:c, :], pT_hi[0:CR, 0:c, cols].bitcast(F32),
                                  ALU.subtract).then_inc(pT_lo_ready, 1)

            def end_low(i):
                cols = slice((TILES - 2 + i) * P, (TILES - 1 + i) * P)
                for k in range(BANKS):
                    dve.wait_ge(end_hi_ready, BANKS * i + k + 1)
                    c = slice(k * CB, (k + 1) * CB)
                    dve.tensor_tensor(pT_lo[0:CR, c, cols], probsT[0:CR, c, :], pT_hi[0:CR, c, cols].bitcast(F32),
                                      ALU.subtract).then_inc(end_lo_ready, 1)

            def late_low(g, u):
                dve.wait_ge(late_hi_ready, NB * g + (u - 2) // TILES + 1)
                cols = slice(TA * P, (TA + 1) * P)
                dve.tensor_tensor(pT_lo[0:CR, LATE_C:CH, cols], probsT[0:CR, LATE_C:CH, :],
                                  pT_hi[0:CR, LATE_C:CH, cols].bitcast(F32), ALU.subtract).then_inc(late_lo_ready, 1)

            def split_high(batch, par):
                dve.wait_ge(ctx_loaded, 16 * (batch + 1))
                wait(dve, attn_ready, 2 * (batch - 1))
                dve.tensor_copy(ctx_hi[0:CR, par, :, :], raw[0:CR, :, :]).then_inc(ctx_split, 1)

            fin = [0, 0]

            def step(ins):
                fin[1] += 1
                ins.then_inc(finish_step, 1)

            def chain(ins):
                step(ins)
                dve.wait_ge(finish_step, FINISH_OPS * fin[0] + fin[1])

            def moments(src):
                chain(dve.bn_stats(stats[0:GR, 0, :], src))
                dve.memset(f[0:GR, 15:16], 0.0)
                chain(dve.bn_aggr(f[0:GR, 0:2], stats[0:GR, 0, :]))
                dve.tensor_scalar(ve[0:GR, 0:1], f[0:GR, 1:2], EPS, None, ALU.add).then_inc(root_asked, 1)

            def stable_norm(bank):
                o = bank[0:GR, 0:D]
                chain(dve.tensor_reduce(f[0:GR, 2:3], o, AX.X, ALU.max))
                chain(dve.reciprocal(f[0:GR, 3:4], f[0:GR, 2:3]))
                dve.tensor_scalar(z[0:GR, :], o, f[0:GR, 3:4], None, ALU.mult).then_inc(side_drained, 1)

            def norm_moments(n):
                dve.wait_ge(side_drained, n + 1)
                moments(z[0:GR, :])

            def residual(grp):
                chain(dve.scalar_tensor_tensor(z[0:GR, :], z[0:GR, :], f[0:GR, 0:1], gout[0:GR, :],
                                               ALU.subtract, ALU.mult))
                dve.wait_ge(root_done, 2 + 2 * grp + 1)
                chain(dve.scalar_tensor_tensor(x2[0:GR, :], z[0:GR, :], rstd[0:GR, 0:1], row(xin, grp),
                                               ALU.mult, ALU.add))
                moments(x2[0:GR, :])

            def centre():
                chain(dve.tensor_scalar(z[0:GR, :], x2[0:GR, :], f[0:GR, 0:1], None, ALU.subtract))
                chain(dve.tensor_reduce(f[0:GR, 2:3], z[0:GR, :], AX.X, ALU.max, apply_absolute_value=True))

            def quantise_rows(grp):
                dve.wait_ge(root_done, 2 + 2 * grp + 2)
                chain(dve.tensor_scalar(f[0:GR, 6:7], f[0:GR, 2:3], rstd[0:GR, 0:1], EPS, ALU.mult, ALU.max))
                chain(dve.tensor_scalar(f[0:GR, 7:8], f[0:GR, 6:7], 1.0 / 127.0, None, ALU.mult))
                dve.reciprocal(f[0:GR, 3:4], f[0:GR, 7:8]).then_inc(rounding_asked, 1)

            def hidden_size():
                chain(dve.tensor_reduce(f[0:GR, 2:3], hidden, AX.X, ALU.max, apply_absolute_value=True))

            def quantise_hidden():
                chain(dve.tensor_scalar(f[0:GR, 7:8], f[0:GR, 2:3], EPS, 1.0 / 127.0, ALU.max, ALU.mult))
                dve.reciprocal(f[0:GR, 3:4], f[0:GR, 7:8]).then_inc(rounding_asked, 1)
                step(dve.tensor_scalar(f[0:GR, 8:9], wmean[0:GR, 2:3], f[0:GR, 7:8], None, ALU.mult))

            def end_round_rows():
                dve.wait_ge(rounding_asked, 2 * GROUPS - 1)
                chain(dve.tensor_scalar(z[0:GR, :], z[0:GR, :], rstd[0:GR, 0:1], f[0:GR, 3:4], ALU.mult, ALU.mult))
                chain(dve.tensor_scalar(z[0:GR, :], z[0:GR, :], ROUND, None, ALU.add))
                dve.tensor_scalar(yq[0:GR, :], z[0:GR, :], ROUND, None, ALU.subtract).then_inc(rows_quantised, 1)
                chain(dve.tensor_scalar(f[0:GR, 4:5], wmean[0:GR, 0:1], f[0:GR, 7:8], 0.5, ALU.mult, ALU.mult))
                dve.tensor_scalar(f[0:GR, 5:6], wmean[0:GR, 1:2], f[0:GR, 7:8], f[0:GR, 4:5],
                                  ALU.mult, ALU.mult).then_inc(scales_ready, 1)

            def end_round_hidden():
                dve.wait_ge(rounding_asked, 2 * GROUPS)
                chain(dve.tensor_scalar(hidden, hidden, f[0:GR, 3:4], ROUND, ALU.mult, ALU.add))
                dve.tensor_scalar(ff_q[0:GR, :], hidden, ROUND, None, ALU.subtract).then_inc(rows_quantised, 1)

            def finish_between(u, o_step):
                if u == 8:
                    norm_moments(o_step)
                elif u == 9:
                    centre()
                elif u == 12:
                    quantise_hidden()

            def finish_after(u, grp):
                if u == 8:
                    residual(grp)
                elif u == 9:
                    quantise_rows(grp)
                elif u == 11:
                    hidden_size()

            def low_ctxT(k, par, bank, drained):
                cols = slice(k * BANK, (k + 1) * BANK)
                dve.tensor_tensor(ctxT_lo[:, par, cols], bank[:, 0:BANK], ctxT_hi[:, par, cols].bitcast(F32),
                                  ALU.subtract).then_inc(drained, 1)

            def low_qk(k, bank, drained):
                e, h = k // 2, HEADS * (k % 2)
                src = bank[:, 0:HEADS * GR].rearrange("p (h j t i) -> p h j t i", h=HEADS, j=NB, i=QT)
                dve.tensor_tensor(by_head(qk_lo[:, 0, :], e)[:, h:h + HEADS], src[:, :, 0],
                                  by_head(qk_hi[:, 0, :], e)[:, h:h + HEADS].bitcast(F32), ALU.subtract
                                  ).then_inc(drained, 1)

            def split_high_qk(g):
                dve.wait_ge(qk_stashed, 4 * (g + 1))
                dve.tensor_copy(qk_hi[:, 1, :], qk_next[:]).then_inc(qk_split, 1)

            def side_step(name, sides, g, par, kind=""):
                n, r = sides.take(name)
                bank = side_bank(kind, name)
                grp = g - 1
                if name in SPLIT:
                    dve.wait_ge(side_rounded, r + 1)
                    if name[0] == "c":
                        low_ctxT(int(name[2]), par, side, side_drained)
                    else:
                        dve.wait_ge(qk_stashed, 4 * (g + 1) + int(name[2]) + 1)
                        low_qk(int(name[2]), side, side_drained)
                elif name == "wsum":
                    dve.wait_ge(side_filled, n + 1)
                    dve.tensor_scalar(wmean[:], side[:, 0:3], 1.0 / (FF * D), EPS, ALU.mult, ALU.max
                                      ).then_inc(side_drained, 1)
                    dve.wait_ge(side_drained, n + 1)
                    dve.reciprocal(wscale[:], wmean[:]).then_inc(scales_found, 1)
                elif name in ("nvoT", "nvo"):
                    dve.wait_ge(side_filled, n + 1)
                    dve.tensor_copy(nvo[:], side[:, 0:D]).then_inc(side_drained, 1)
                elif name == "u0":
                    dve.wait_ge(probs_ready, 2 * SLOTS * g)
                    cols = null_probs[:, SLOTS * grp:SLOTS * g] if isinstance(grp, int) else \
                        null_probs[:, bass.ds(grp * SLOTS, SLOTS)]
                    dve.tensor_tensor(null_sel[:], cols.unsqueeze(2).broadcast_to((P, SLOTS, QT)),
                                      sel[:].unsqueeze(1).broadcast_to((P, SLOTS, QT)), ALU.mult
                                      ).then_inc(null_sel_ready, 1)
                elif name == "o":
                    fin[0], fin[1] = grp, 0
                    dve.wait_ge(side_filled, n + 1)
                    stable_norm(bank)
                elif name == "gate":
                    dve.wait_ge(side_tanh, grp + 1)
                    dve.scalar_tensor_tensor(hidden, hidden, 1.0, side[0:GR, :], ALU.add, ALU.mult
                                             ).then_inc(side_drained, 1)
                elif name == "up":
                    dve.wait_ge(side_filled, n + 1)
                    if kind == "end":
                        dve.wait_ge(side_drained, n)
                    dve.scalar_tensor_tensor(hidden, hidden, f[0:GR, 5:6], bank[0:GR, :], ALU.mult, ALU.mult
                                             ).then_inc(side_drained, 1)
                    dve.wait_ge(side_drained, n + 1)
                elif name == "down":
                    dve.wait_ge(side_filled, n + 1)
                    if isinstance(grp, int):
                        wait(dve, out_written, 16 * grp)
                    dve.wait_ge(finish_step, FINISH_OPS * grp + fin[1])
                    dve.scalar_tensor_tensor(result[0:GR, :], side[0:GR, 0:D], f[0:GR, 8:9], x2[0:GR, :],
                                             ALU.mult, ALU.add).then_inc(side_drained, 1)

            def clip_weights(k):
                dve.wait_ge(weights_rounded, k + 1)
                if k > 0:
                    dve.wait_ge(side_filled, steps_of("first").index(("wgT", "wuT")[k - 1]) + 1)
                dve.tensor_scalar(ff_q[:], raw_ffn[:, k * FF:(k + 1) * FF], 1.0, -1.0, ALU.min, ALU.max
                                  ).then_inc(weights_quantised, 1)

            def group(kind, g):
                sides = Sides(kind, g)
                o_step = sides.base + (steps_of(kind).index("o") if kind != "first" else 0)
                for u in range(SLOTS):
                    j, v = divmod(u, TILES)
                    max_banks(g, u)
                    for name in steps_at(kind, u, 0):
                        side_step(name, sides, g, (j + 1) % 2)
                    if kind != "first":
                        finish_between(u, o_step)
                    max_last(g, u)
                    if "up" in steps_at(kind, u, 1):
                        side_step("up", sides, g, (j + 1) % 2)
                    if kind != "first" or u >= 2:
                        low_part(g, u)
                    for name in steps_at(kind, u, 1):
                        if name in SPLIT:
                            side_step(name, sides, g, (j + 1) % 2)
                    invert_sums(g, u)
                    if v == TA + 2:
                        late_low(g, u)
                    if u == 1:
                        split_high_qk(g)
                    if v == TILES - 1 and not (kind == "last" and j == NB - 1):
                        split_high(NB * g + j + 1, (j + 1) % 2)
                    for name in steps_at(kind, u, 1):
                        if name not in SPLIT and name != "up":
                            side_step(name, sides, g, (j + 1) % 2)
                    if kind != "first":
                        finish_after(u, g - 1)
                    elif u in (4, 5, 6):
                        clip_weights(u - 4)
                assert kind == "first" or fin[1] == FINISH_OPS, fin[1]

            steps = [0]

            def start_chain(instructions):
                for ins in instructions:
                    steps[0] += 1
                    ins.then_inc(start_step, 1)
                dve.wait_ge(start_step, steps[0])

            def start_moments(src):
                start_chain([dve.bn_stats(stats[0:GR, k, :], src[0:GR, k, :]) for k in range(GROUPS)])
                start_chain([dve.bn_aggr(mv[0:GR, k, :], stats[0:GR, k, :]) for k in range(GROUPS)])
                dve.tensor_scalar(ve[0:GR, :], mv[0:GR, :, 1], EPS, None, ALU.add).then_inc(root_asked, 1)

            dve.wait_ge(x_loaded, 16)
            start_moments(xin)
            dve.wait_ge(root_done, 1)
            start_chain([dve.tensor_scalar(xw[:, k, :], xin[0:GR, k, :], mv[0:GR, k, 0:1], rstd[0:GR, k:k + 1],
                                           ALU.subtract, ALU.mult) for k in range(GROUPS)])
            start_chain([dve.tensor_reduce(row_max[0:GR, :], xw, AX.X, ALU.max)])
            start_chain([dve.reciprocal(ve[0:GR, :], row_max[0:GR, :])])
            start_chain([dve.tensor_scalar(xw[:, k, :], xw[:, k, :], ve[0:GR, k:k + 1], None, ALU.mult)
                         for k in range(GROUPS)])
            start_moments(xw)
            dve.wait_ge(ident_loaded, 16)
            dve.tensor_copy(ident16[:], ident[:]).then_inc(xn_ready, 1)
            dve.wait_ge(null_weighted, 1)
            dve.tensor_reduce(wnk, wq_null, AX.X, ALU.add).then_inc(wnk_ready, 1)
            dve.wait_ge(root_done, 2)
            for k in range(GROUPS):
                dve.tensor_scalar(xw[:, k, :], xw[:, k, :], mv[0:GR, k, 0:1], rstd[0:GR, k:k + 1],
                                  ALU.subtract, ALU.mult).then_inc(xn_ready, 1)
            names = [name for _, name, _ in START]
            for n in map(names.index, VECTOR_ORDER):
                lane, name, bank = START[n]
                src = bank_of(bank)
                if lane == "read":
                    dve.wait_ge(start_filled, n + 1)
                if name == "xT":
                    dve.wait_ge(small_loaded, SMALL)
                    dve.tensor_scalar(xnT[:], src[:, 0:GROUPS * GR], gin[:, 0:1], None, ALU.mult
                                      ).then_inc(start_read, 1)
                elif name == "n0":
                    dve.tensor_scalar(n0, src[0:H, 0:GROUPS * GR], SCALE, None, ALU.mult).then_inc(start_read, 1)
                elif name == "n1":
                    slots = GROUPS * SLOTS
                    dve.tensor_tensor(null_rows, src[:, 0:GROUPS * GR].rearrange("p (s i) -> p s i", i=QT),
                                      sel[:].unsqueeze(1).broadcast_to((P, slots, QT)), ALU.mult
                                      ).then_inc(start_read, 1)
                    dve.wait_ge(start_read, 3)
                    dve.tensor_reduce(null_scores[:], null_rows, AX.X, ALU.add).then_inc(start_read, 1)
                elif lane == "split":
                    k = int(name[-1])
                    dve.wait_ge(start_rounded, k + 1 if name[0] == "c" else 3 + k + 1)
                    if name[0] == "c":
                        low_ctxT(k, 0, src, start_split)
                    else:
                        dve.wait_ge(qk_stashed, k + 1)
                        low_qk(k, src, start_split)
            group("first", 0)
            with dve.Fori(1, GROUPS - 1) as g:
                group("middle", g)
            group("last", GROUPS - 1)
            for i in range(2):
                end_low(i)
            sides = Sides("end", GROUPS)
            for _, _, name in FINISH:
                if name == "xt":
                    norm_moments(sides.base + sides.n - 1)
                    residual(GROUPS - 1)
                    centre()
                    quantise_rows(GROUPS - 1)
                    end_round_rows()
                if name == "ht":
                    hidden_size()
                    quantise_hidden()
                    end_round_hidden()
                side_step(name, sides, GROUPS, 0, "end")

        @block.tensor
        def _(pe):
            def three_passes(out_ap, high, low, m_high, m_low, start, stop):
                nc.tensor.matmul(out_ap, high, m_high, start=start, stop=False)
                nc.tensor.matmul(out_ap, high, m_low, start=False, stop=False)
                return nc.tensor.matmul(out_ap, low, m_high, start=False, stop=stop)

            def score_banks(kind, g, u, banks, prepared_at):
                j, v = divmod(u, TILES)
                s, par = SLOTS * g + u, j % 2
                if v == 0:
                    wait(pe, side_drained, prepared_at - (j == 0 and 0 in banks))
                    if j == 1 and 0 in banks:
                        pe.wait_ge(qk_split, 2 * g + 2)
                cols = slice(v * P, (v + 1) * P)
                for k in banks:
                    wait(pe, exp_done, BANKS * (s - 1) + k + 1)
                    keys = slice(k * BANK, (k + 1) * BANK)
                    at = last_bank_at(v) if k == BANKS - 1 else 0
                    if k == BANKS - 1 and kind == "first" and u == 0:
                        pe.wait_ge(start_read, 4)
                    if k == BANKS - 1 and at == 0:
                        n = min(AHEAD, TILES - v)
                        nc.tensor.matmul(scores[:, k, BANK:BANK + 2 * n - 1:2], ident[:],
                                         null_scores[:, s:s + n] if isinstance(s, int) else
                                         null_scores[:, bass.ds(s, n)], start=True, stop=True)
                    last = three_passes(scores[:, k, at:at + BANK], qk_hi[:, par, cols], qk_lo[:, par, cols],
                                        ctxT_hi[:, par, keys], ctxT_lo[:, par, keys], True, True)
                last.then_inc(scores_ready, 1)

            def transpose_probs(g, u):
                s, par = SLOTS * g + u - 2, u % 2
                j, v = divmod(u, TILES)
                pe.wait_ge(probs_ready, 2 * (s + 1))
                wait(pe, pT_lo_ready, s)
                for c in range(CH):
                    if c == LATE_C and v == TA + 3:
                        pe.wait_ge(late_lo_ready, NB * g + j + 1)
                    last = nc.tensor.transpose(probsT[0:CR, c, :], probs[:, par, c * CR:(c + 1) * CR], ident[:])
                last.then_inc(probsT_ready, 1)

            def probs_by_ctx(kind, g, u):
                j, v = divmod(u, TILES)
                if v == TILES - 1:
                    b, jb, first, part, parts = NB * g + j, j, True, 0, 3
                elif v < 2:
                    b, jb, first, part, parts = NB * g + j - 1, j - 1, True, v + 1, 3
                else:
                    b, jb, first, part, parts = NB * g + j - 1, j - 1, False, v - 2, 4
                par = jb % 2
                lo, hi = part_columns(kind if u >= SLOTS - 1 else "", jb % 2, not first)
                tiles = hi // P
                if part == 0:
                    pe.wait_ge(pT_lo_ready, SLOTS * g + TILES * (j - (not first)) + tiles)
                    wait(pe, attn_drained, 2 * b + (not first))
                    pe.wait_ge(ctx_split, 2 * (b + 1))
                per = CH // parts
                for c in range(part * per, (part + 1) * per):
                    pairs = ((ctx_hi, pT_hi), (ctx_lo, pT_hi), (ctx_hi, pT_lo))
                    for i, (w, m) in enumerate(pairs):
                        last = nc.tensor.matmul(attn[:, 0:hi - lo], w[0:CR, par, c, :], m[0:CR, c, lo:hi],
                                                start=(c == 0 and i == 0), stop=(c == CH - 1 and i == 2))
                if part == parts - 1:
                    last.then_inc(attn_ready, 1)

            def end_transposes(i):
                s = GROUPS * SLOTS - 2 + i
                pe.wait_ge(probs_ready, 2 * (s + 1))
                if i == 0:
                    pe.wait_ge(pT_lo_ready, s)
                for c in range(CH):
                    if i > 0 and c % CB == 0:
                        pe.wait_ge(end_lo_ready, c // CB + 1)
                    last = nc.tensor.transpose(probsT[0:CR, c, :], probs[:, s % 2, c * CR:(c + 1) * CR], ident[:])
                    if c % CB == CB - 1:
                        last.then_inc(end_transposed, 1)

            def end_probs_by_ctx():
                lo, hi = part_columns("last", NB - 1, True)
                par = (B - 1) % 2
                pe.wait_ge(end_hi_ready, 2 * BANKS)
                for c in range(CH):
                    for w in (ctx_hi, ctx_lo):
                        nc.tensor.matmul(scores[:, 0, 0:hi - lo], w[0:CR, par, c, :], pT_hi[0:CR, c, lo:hi],
                                         start=(c == 0 and w is ctx_hi), stop=False)
                pe.wait_ge(end_lo_ready, 2 * BANKS)
                for c in range(CH):
                    last = nc.tensor.matmul(scores[:, 0, 0:hi - lo], ctx_hi[0:CR, par, c, :], pT_lo[0:CR, c, lo:hi],
                                            start=False, stop=(c == CH - 1))
                last.then_inc(attn_ready, 1)

            def transpose_ctx(k, bank):
                for i in range(CB):
                    last = nc.tensor.transpose(bank[:, i * CR:(i + 1) * CR], raw[0:CR, CB * k + i, :],
                                               ident[0:CR, 0:CR])
                return last

            def fold_queries(k, rows, bank):
                for i in range(HEADS):
                    last = nc.tensor.matmul(bank[:, i * GR:(i + 1) * GR], fold[:, HEADS * k + i, :], rows, start=True, stop=True)
                return last

            def side_step(name, sides, g, j, kind=""):
                n, _ = sides.take(name)
                bank = side_bank(kind, name)
                if kind != "end" or name not in APART:
                    wait(pe, side_drained, n)
                if name in ("ct0", "ct1", "ct2"):
                    pe.wait_ge(ctx_loaded, 16 * (NB * g + j + 2))
                    last = transpose_ctx(int(name[2]), side)
                elif name[0:2] == "qk":
                    at = GR * (g + 1)
                    last = fold_queries(int(name[2]), xnT[:, at:at + GR] if isinstance(at, int) else
                                        xnT[:, bass.ds(at, GR)], side)
                elif name in ("u0", "u1"):
                    k = int(name[1])
                    if k == 0:
                        pe.wait_ge(attn_drained, 2 * NB * g)
                    for h in range(4 * k, 4 * k + 4):
                        for e in range(2):
                            last = nc.tensor.matmul(
                                bank[e * DH:(e + 1) * DH, (h % 4) * GR:(h % 4 + 1) * GR],
                                wv[:, h * P + e * DH:h * P + (e + 1) * DH], attn_by_head[:, :, e, :, h],
                                start=True, stop=True)
                elif name == "o":
                    pe.wait_ge(null_sel_ready, g)
                    nc.tensor.matmul(bank[0:GR, 0:D], null_sel[:].rearrange("p s i -> p (s i)"), nvo[:],
                                     start=True, stop=False)
                    for h in range(PAIRS):
                        if kind == "end" and h % 4 == 0:
                            pe.wait_ge(side_drained, n - 1 + h // 4)
                        last = nc.tensor.matmul(bank[0:GR, 0:D], uT[:, h, :], wo[:, h, :],
                                                start=False, stop=(h == PAIRS - 1))
                elif name == "xt":
                    pe.wait_ge(rows_quantised, 2 * g - 1)
                    last = nc.tensor.transpose(side16[:, 0:GR], yq[0:GR, :], ident16[0:GR, 0:GR])
                elif name in ("gate", "up"):
                    w = ff_gate if name == "gate" else ff_up
                    last = nc.tensor.matmul(bank[0:GR, :], yqT[:, 0:GR], w[:], start=True, stop=True)
                elif name == "ht":
                    pe.wait_ge(rows_quantised, 2 * g)
                    for k in range(FF // P):
                        last = nc.tensor.transpose(side16[:, k * P:k * P + GR], ff_q[0:GR, k * P:(k + 1) * P],
                                                   ident16[0:GR, 0:GR])
                elif name == "down":
                    for k in range(FF // P):
                        last = nc.tensor.matmul(side[0:GR, 0:D], hqT[:, k, 0:GR], ff_down[:, k * P:(k + 1) * P],
                                                start=(k == 0), stop=(k == FF // P - 1))
                elif name == "wsum":
                    pe.wait_ge(weights_summed, 3)
                    last = nc.tensor.matmul(side[:, 0:3], ones[:], wabs[:], start=True, stop=True)
                elif name in ("wgT", "wuT", "wdT"):
                    pe.wait_ge(weights_quantised, 1 + ("wgT", "wuT", "wdT").index(name))
                    for k in range(FF // P):
                        last = nc.tensor.transpose(side16[:, k * P:(k + 1) * P], ff_q[:, k * P:(k + 1) * P],
                                                   ident16[:])
                elif name == "nvoT":
                    pe.wait_ge(window_set, 1)
                    for h in range(PAIRS):
                        last = nc.tensor.matmul(side[:, 0:P], wo[:, h, :],
                                                window[:, :, PAIRS - 1 - h:2 * PAIRS - 1 - h],
                                                start=(h == 0), stop=(h == PAIRS - 1))
                elif name == "nvo":
                    last = nc.tensor.transpose(side[:, 0:D], nvo[:], ident[:])
                last.then_inc(side_filled, 1)

            def keep_warm(n):
                for _ in range(n):
                    nc.tensor.matmul(attn[:, 0:P], ones[:], ones[:], start=True, stop=True)

            def group(kind, g):
                sides = Sides(kind, g)
                prepared_at = sides.base
                for u in range(SLOTS):
                    j, v = divmod(u, TILES)
                    score_banks(kind, g, u, (0, 1), prepared_at)
                    for name in steps_at(kind, u, 0):
                        side_step(name, sides, g, j)
                    if kind != "first" or u >= 2:
                        transpose_probs(g, u)
                    score_banks(kind, g, u, (2,), prepared_at)
                    for name in steps_at(kind, u, 1):
                        side_step(name, sides, g, j)
                    if "ct2" in steps_at(kind, u, 0) + steps_at(kind, u, 1):
                        prepared_at = sides.base + sides.n
                    if kind != "first" or u >= TILES - 1:
                        probs_by_ctx(kind, g, u)
                    else:
                        keep_warm(WARM_SLOT)

            pe.wait_ge(constants_set, 2)
            keep_warm(WARM)
            lanes = {"copy": 0, "read": 0, "split": 0}
            for n, (lane, name, bank) in enumerate(START):
                done, banks = {"copy": (start_copied, 3), "read": (start_read, 2), "split": (start_split, 3)}[lane]
                if name not in ("qk0", "qk1", "qk2"):
                    wait(pe, done, lanes[lane] - banks + 1)
                lanes[lane] += 1
                out_bank = bank_of(bank)
                k = int(name[-1]) if name[-1].isdigit() else 0
                if name[0:3] in ("wqT", "wkT"):
                    w, loaded = (wq, wq_loaded) if name[1] == "q" else (wk, wk_loaded)
                    pe.wait_ge(loaded, 16)
                    if n == 0:
                        pe.wait_ge(ident_loaded, 16)
                    for i in range(4):
                        c = (4 * k + i) * P
                        last = nc.tensor.transpose(out_bank[:, i * P:(i + 1) * P], w[:, c:c + P], ident[:])
                elif name[0:2] == "wf":
                    if k == 0:
                        pe.wait_ge(start_copied, 4)
                    for i in range(4):
                        e, hp = divmod(4 * k + i, PAIRS)
                        half = slice(e * DH, (e + 1) * DH)
                        last = nc.tensor.matmul(out_bank[:, i * P:(i + 1) * P], wqT[half, hp, :], wkT[half, hp, :],
                                                start=True, stop=True)
                elif name[0:2] == "ct":
                    pe.wait_ge(ctx_loaded, 16)
                    last = transpose_ctx(k, out_bank)
                elif name == "xT":
                    pe.wait_ge(xn_ready, 1 + GROUPS)
                    for i in range(GROUPS):
                        last = nc.tensor.transpose(out_bank[:, i * GR:(i + 1) * GR], xw[:, i, :],
                                                   ident[0:GR, 0:GR])
                elif name == "n0":
                    pe.wait_ge(wnk_ready, 1)
                    last = nc.tensor.matmul(out_bank[0:H, 0:GROUPS * GR], wnk, xnT[:], start=True, stop=True)
                elif name == "n1":
                    pe.wait_ge(start_read, 2)
                    pe.wait_ge(small_loaded, SMALL)
                    last = nc.tensor.matmul(out_bank[:, 0:GROUPS * GR], head_rows, n0, start=True, stop=True)
                else:
                    if k == 0:
                        pe.wait_ge(start_copied, 8)
                        pe.wait_ge(start_read, 1)
                    last = fold_queries(k, xnT[:, 0:GR], out_bank)
                last.then_inc(start_filled, 1)
            pe.wait_ge(start_split, 7)
            group("first", 0)
            with pe.Fori(1, GROUPS - 1) as g:
                group("middle", g)
            group("last", GROUPS - 1)
            for i in range(2):
                end_transposes(i)
                probs_by_ctx("last", GROUPS - 1, SLOTS + i)
            end_probs_by_ctx()
            sides = Sides("end", GROUPS)
            for _, _, name in FINISH:
                side_step(name, sides, GROUPS, 0, "end")


_INS = ["x", "ctx_1024", "L0_xattn_Wq", "L0_xattn_Wkv", "L0_xattn_Wo", "L0_xattn_g_in", "L0_xattn_g_out",
        "L0_xattn_null_kv", "L0_ffn_w_gate", "L0_ffn_w_up", "L0_ffn_w_down"]


def kernel(**inputs):
    import numpy as _np
    import concourse.bacc as _bacc
    from concourse import mybir as _mybir
    from concourse.bass_utils import run_bass_kernel_spmd as _run

    nc = _bacc.Bacc("TRN2", target_bir_lowering=False, num_devices=1)
    arrays = {n: _np.ascontiguousarray(inputs[n]) for n in _INS}
    r = _np.arange(P)
    arrays["identity"] = _np.eye(P, dtype=_np.float32)
    arrays["query_of"] = (((r % DH) // PAIRS)[:, None] == _np.arange(QT)[None, :]).astype(_np.float32)
    window = _np.zeros((P, 2, QT, 15), _np.float32)
    window[0:DH, 0, :, PAIRS - 1] = 1.0
    window[DH:P, 1, :, PAIRS - 1] = 1.0
    arrays["head_window"] = window.reshape(P, 16, 15)
    arrays["head_of"] = (_np.arange(H)[:, None] == (2 * (r % PAIRS) + r // DH)[None, :]).astype(_np.float32)
    args = [nc.dram_tensor(f"in_{n}_dram", a.shape, _mybir.dt.from_np(a.dtype), kind="ExternalInput").ap()
            for n, a in arrays.items()]
    out = nc.dram_tensor("out_0_dram", (B, N, D), _mybir.dt.float32, kind="ExternalOutput").ap()
    build(nc, *args, out)
    got = _run(nc, [{f"in_{n}_dram": a for n, a in arrays.items()}], core_ids=[0])
    return got.results[0]["out_0_dram"]
```
